# Optimizing a Trainium2 kernel written in Bass

```python
import numpy as np
import jax
import jax.numpy as jnp

def _softmax(x, axis=-1):
    return jax.nn.softmax(x, axis=axis)

def _gelu(x):
    return jax.nn.gelu(x, approximate=True)

def _silu(x):
    return jax.nn.silu(x)

def _sigmoid(x):
    return jax.nn.sigmoid(x)

def _layernorm(x, axis=-1, eps=1e-05):
    m = jnp.mean(x, axis=axis, keepdims=True)
    v = jnp.var(x, axis=axis, keepdims=True)
    return (x - m) / jnp.sqrt(v + eps)

def _scatter_add(tgt, idx, src, axis=0):
    return tgt.at[idx].add(src)

def _segment_sum(src, seg, n):
    return jax.ops.segment_sum(src, seg, n)
kernel_name = 'mk_gnn_resnorm_d2_gnn_r16_cf1a6d'

def setup_inputs(seed: int=0):
    np.random.seed(seed)
    _w = jnp.asarray

    def _rec_inputs():
        import jax
        import jax.numpy as jnp
        _gk = jax.random.key(seed)
        x = -0.000202 + 1 * jax.random.normal(jax.random.fold_in(_gk, 1), (6250, 128), jnp.float32)
        src = jax.random.randint(jax.random.fold_in(_gk, 2), (200000,), 0, 6250, jnp.int32)
        dst = jax.random.randint(jax.random.fold_in(_gk, 3), (200000,), 0, 6250, jnp.int32)
        _o = jnp.argsort(dst, stable=True)
        src = src[_o]
        dst = dst[_o]
        edge_type_8 = jax.random.randint(jax.random.fold_in(_gk, 13), (200000,), 0, 8, jnp.int32)
        node_type_4 = jax.random.randint(jax.random.fold_in(_gk, 14), (6250,), 0, 4, jnp.int32)
        return (x, src, dst, edge_type_8, node_type_4)
    x, src, dst, edge_type_8, node_type_4 = _rec_inputs()

    def _L0_gnn_setup():
        import jax, jax.numpy as jnp
        import numpy as np
        N_NODES = 3125
        N_EDGES = 37500
        D = 128
        key = jax.random.key(seed)
        k1, k2, k3, k4, k5 = jax.random.split(key, 5)
        x = jax.random.normal(k1, (N_NODES, D), dtype=jnp.float32)
        W = jax.random.normal(k2, (D, 2 * D), dtype=jnp.float32) * (1.0 / np.sqrt(2 * D))
        b = jax.random.normal(k3, (D,), dtype=jnp.float32) * 0.01
        src = jax.random.randint(k4, (N_EDGES,), 0, N_NODES, dtype=jnp.int32)
        dst = jax.random.randint(k5, (N_EDGES,), 0, N_NODES, dtype=jnp.int32)
        return {'x': x, 'W': W, 'b': b, 'src': src, 'dst': dst}
    _L0_gnn_all = _L0_gnn_setup()
    _L0_gnn_in = {k: v for k, v in _L0_gnn_all.items() if k in ('W', 'b')}
    del _L0_gnn_all

    def _L1_gnn_setup():
        import jax, jax.numpy as jnp
        import numpy as np
        import math
        HIDDEN = 128
        N_NODES = 3125
        N_EDGES = 50000
        N_NTYPES = 4
        N_ETYPES = 8

        def _type_matmul(h, W, types):
            out = jnp.zeros_like(h)
            for t in range(W.shape[0]):
                out = out + jnp.where((types == t)[:, None], h @ W[t], 0.0)
            return out

        def _sparse_softmax(scores, indices, n_segments):
            seg_max = jnp.maximum(jax.ops.segment_max(scores, indices, num_segments=n_segments), -1000000000.0)
            exp_s = jnp.exp(scores - seg_max[indices])
            seg_sum = jax.ops.segment_sum(exp_s, indices, num_segments=n_segments)
            return exp_s / (seg_sum[indices] + 1e-10)
        key = jax.random.key(seed)
        ks = jax.random.split(key, 10)
        x = jax.random.normal(ks[0], (N_NODES, HIDDEN), dtype=jnp.float32)
        edge_index = jax.random.randint(ks[1], (2, N_EDGES), 0, N_NODES, dtype=jnp.int64 if jax.config.read('jax_enable_x64') else jnp.int32)
        edge_type = jax.random.randint(ks[2], (N_EDGES,), 0, N_ETYPES, dtype=jnp.int32)
        node_type = jax.random.randint(ks[3], (N_NODES,), 0, N_NTYPES, dtype=jnp.int32)
        W_Q = jax.random.normal(ks[4], (N_NTYPES, HIDDEN, HIDDEN), dtype=jnp.float32) * 0.02
        W_K = jax.random.normal(ks[5], (N_NTYPES, HIDDEN, HIDDEN), dtype=jnp.float32) * 0.02
        W_V = jax.random.normal(ks[6], (N_NTYPES, HIDDEN, HIDDEN), dtype=jnp.float32) * 0.02
        W_edge = jax.random.normal(ks[7], (N_ETYPES, HIDDEN, HIDDEN), dtype=jnp.float32) * 0.02
        mu = jnp.ones((N_ETYPES,), dtype=jnp.float32)
        return {'x': x, 'edge_index': edge_index, 'edge_type': edge_type, 'node_type': node_type, 'W_Q': W_Q, 'W_K': W_K, 'W_V': W_V, 'W_edge': W_edge, 'mu': mu}
    _L1_gnn_all = _L1_gnn_setup()
    _L1_gnn_in = {k: v for k, v in _L1_gnn_all.items() if k in ('W_Q', 'W_K', 'W_V', 'W_edge', 'mu')}
    del _L1_gnn_all
    return {'x': x, 'src': src, 'dst': dst, 'edge_type_8': edge_type_8, 'node_type_4': node_type_4, 'L0_gnn_W': _L0_gnn_in['W'], 'L0_gnn_b': _L0_gnn_in['b'], 'L1_gnn_W_Q': _L1_gnn_in['W_Q'], 'L1_gnn_W_K': _L1_gnn_in['W_K'], 'L1_gnn_W_V': _L1_gnn_in['W_V'], 'L1_gnn_W_edge': _L1_gnn_in['W_edge'], 'L1_gnn_mu': _L1_gnn_in['mu']}

def reference(x, src, dst, edge_type_8, node_type_4, L0_gnn_W, L0_gnn_b, L1_gnn_W_Q, L1_gnn_W_K, L1_gnn_W_V, L1_gnn_W_edge, L1_gnn_mu):
    import jax
    import jax.numpy as jnp

    def _L0_gnn_ref(x, W, b, src, dst):
        import jax, jax.numpy as jnp
        import numpy as np
        N_NODES = 3125
        N_EDGES = 37500
        D = 128
        N = x.shape[0]
        neigh_sum = jax.ops.segment_sum(x[src], dst, num_segments=N)
        deg = jax.ops.segment_sum(jnp.ones_like(src, dtype=x.dtype), dst, num_segments=N)
        mean = neigh_sum / jnp.maximum(deg, 1.0)[:, None]
        neigh_agg = jnp.where(deg[:, None] > 0, mean, x)
        h = jnp.concatenate([x, neigh_agg], axis=-1)
        return jax.nn.relu(h @ W.T + b)

    def _L1_gnn_ref(x, edge_index, edge_type, node_type, W_Q, W_K, W_V, W_edge, mu):
        import jax, jax.numpy as jnp
        import numpy as np
        import math
        HIDDEN = 128
        N_NODES = 3125
        N_EDGES = 50000
        N_NTYPES = 4
        N_ETYPES = 8

        def _type_matmul(h, W, types):
            out = jnp.zeros_like(h)
            for t in range(W.shape[0]):
                out = out + jnp.where((types == t)[:, None], h @ W[t], 0.0)
            return out

        def _sparse_softmax(scores, indices, n_segments):
            seg_max = jnp.maximum(jax.ops.segment_max(scores, indices, num_segments=n_segments), -1000000000.0)
            exp_s = jnp.exp(scores - seg_max[indices])
            seg_sum = jax.ops.segment_sum(exp_s, indices, num_segments=n_segments)
            return exp_s / (seg_sum[indices] + 1e-10)
        N, d = x.shape
        scale = math.sqrt(d)
        src, dst = (edge_index[0], edge_index[1])
        Q = _type_matmul(x, W_Q, node_type)
        K = _type_matmul(x, W_K, node_type)
        V = _type_matmul(x, W_V, node_type)
        q_dst = Q[dst]
        k_src = K[src]
        k_t = _type_matmul(k_src, W_edge, edge_type)
        scores = jnp.sum(q_dst * k_t, axis=-1) / scale
        scores = scores * mu[edge_type]
        attn = _sparse_softmax(scores, dst, N)
        weighted_v = V[src] * attn[:, None]
        out = jax.ops.segment_sum(weighted_v, dst, num_segments=N)
        return out
    edge_index = jnp.stack([src, dst])
    x = _layernorm(x + _L0_gnn_ref(x, L0_gnn_W, L0_gnn_b, src, dst), axis=-1)
    x = _layernorm(x + _L1_gnn_ref(x, edge_index, edge_type_8, node_type_4, L1_gnn_W_Q, L1_gnn_W_K, L1_gnn_W_V, L1_gnn_W_edge, L1_gnn_mu), axis=-1)
    return x

_drawn_inputs = setup_inputs


def setup_inputs(seed=0):
    import zlib

    import numpy as np

    out = dict(_drawn_inputs(seed))
    spreads = {'L1_gnn_mu': (1.0, 0.6)}
    factors = {'L0_gnn_b': 8.0, 'L1_gnn_W_Q': 8.0, 'L1_gnn_W_K': 8.0, 'L1_gnn_W_edge': 8.0}
    for name, (base, spread) in spreads.items():
        noise = np.random.default_rng([zlib.crc32(name.encode()), seed]).standard_normal(out[name].shape)
        drawn = base * np.exp(spread * noise) if base else spread * noise
        out[name] = jnp.asarray(drawn.astype(out[name].dtype))
    for name, factor in factors.items():
        out[name] = (out[name] * factor).astype(out[name].dtype)
    return out
```

```python
from contextlib import ExitStack

import concourse.bass as bass
from concourse import mybir

ALU = mybir.AluOpType
ACT = mybir.ActivationFunctionType
AX = mybir.AxisListType.X
F32 = mybir.dt.float32
BF16 = mybir.dt.bfloat16
I32 = mybir.dt.int32
U32 = mybir.dt.uint32

P = 128
RUN = 8
HALF = P * RUN
BLOCK = 2 * HALF
COLS = 2 * RUN
WIN = 64
SLOTS = 3
NEG = -1.0e30
FLOOR = -1.0e9
LN_EPS = 1e-5
SUM_EPS = 1e-10


def gnn_kernel(nc, x, src, dst, etype, ntype, w0, b0, wq, wk, wv, we, mu, out):
    N, D = x.shape
    E = src.shape[0]
    NT = wq.shape[0]
    ET = we.shape[0]
    assert D == P and NT * D == 512 and ET == 8
    TILES = -(-N // P)
    LAST = N - (TILES - 1) * P
    NPAD = TILES * P
    CH = 7
    CHUNKS = TILES // CH
    CW = CH * P
    assert CHUNKS * CH == TILES
    NBLK = -(-E // BLOCK)
    NHALF = 2 * NBLK
    FULL = E // HALF
    REST = E - FULL * HALF
    assert FULL == NHALF - 1 and REST % RUN == 0 and REST > 0
    NPASS = -(-N // WIN)
    NACC = NPAD + WIN
    TURNS = [-(-(NBLK - u) // SLOTS) for u in range(SLOTS)]
    SCALE = float(D) ** -0.5

    with ExitStack() as ctx:
        def sb(name, shape, dt=F32):
            return ctx.enter_context(nc.sbuf_tensor(name, shape, dt))

        def ps(name, shape, dt=F32):
            return ctx.enter_context(nc.psum_tensor(name, shape, dt))

        def sem(name):
            return ctx.enter_context(nc.semaphore(name))

        table = nc.dram_tensor("kv_table", (NPAD * ET, 2 * D), F32, kind="Internal").ap()
        table_tiles = table.rearrange("(n e) c -> n (e c)", e=ET)
        x1_dram = nc.dram_tensor("x1_rows", (NPAD, D), F32, kind="Internal").ap()
        x1_view = x1_dram.rearrange("(t p) d -> p t d", p=P)

        sums = sb("sums", [P, 2, NACC])
        negmax = sb("negmax", [P, NACC])
        nodes = sb("nodes", [P, NACC])
        src_idx = sb("src_idx", [P, NHALF * RUN], U32)
        key_idx = sb("key_idx", [P, NHALF * RUN], U32)
        dst_f = sb("dst_f", [P, NHALF * RUN])
        rel = sb("rel", [P, NHALF * RUN])
        ring = sb("ring", [P, SLOTS * COLS * 2 * D])
        keysT = sb("keysT", [P, 4, 512])
        probT = sb("probT", [P, HALF])
        prob = sb("prob", [P, RUN, P])
        away = sb("away", [P, COLS, WIN], BF16)
        identf = sb("identf", [P, P])
        identb = sb("identb", [P, P], BF16)
        negid = sb("negid", [P, P], BF16)
        onesf = sb("onesf", [P, P])
        queries = sb("queries", [P, 2, WIN])
        iota_i = sb("iota_i", [P, WIN], I32)
        iota_f = sb("iota_f", [P, WIN])
        first = sb("first", [P, NHALF])
        base_f = sb("base_f", [P, NHALF])
        base_i = sb("base_i", [1, NHALF], I32)
        step_f = sb("step_f", [P, 4])
        passes_i = sb("passes_i", [1, 2], I32)
        cols = sb("cols", [P, 8])
        spread = sb("spread", [P, 2, P])
        delta = sb("delta", [P, 2, WIN])
        factor = sb("factor", [P, 2, WIN])
        scaled = sb("scaled", [P, 2, 2, WIN])
        bias_c = sb("bias_c", [P, 1])
        mu_b = sb("mu_b", [P, ET])
        ntype_i = sb("ntype_i", [P, TILES], I32)
        ntype_m = sb("ntype_m", [P, TILES, NT])
        stats = sb("stats", [P, CH, 6])
        aggr = sb("aggr", [P, CH, 2])
        std = sb("std", [P, CH])
        eps_col = sb("eps_col", [P, 1])
        stage = sb("stage", [P, SLOTS, COLS], U32)

        dst_i = rel[:, :].bitcast(I32)
        etype_i = keysT[:, :, :].rearrange("p a b -> p (a b)").bitcast(I32)[:, 0:NHALF * RUN]
        hot = probT[:, :].rearrange("p (j w) -> p j w", w=WIN)
        x_ring = [ring[:, u * COLS * D:(u + 1) * COLS * D].rearrange("p (j d) -> p j d", d=D) for u in range(SLOTS)]
        kv_ring = [ring[:, u * COLS * 2 * D:(u + 1) * COLS * 2 * D].rearrange("p (j c) -> p j c", c=2 * D)
                   for u in range(SLOTS)]
        x_nodes = nodes[:, 0:NPAD].rearrange("p (t d) -> p t d", d=D)
        at = [0]

        def part(n):
            at[0] += n
            assert at[0] <= SLOTS * COLS * 2 * D
            return ring[:, at[0] - n:at[0]]

        kv_rows = [part(ET * 2 * D).rearrange("p (e c) -> p e c", c=2 * D) for _ in range(2)]
        x1_typed = [part(NT * D).rearrange("p (t d) -> p t d", d=D) for _ in range(2)]
        x1_typedT = [part(NT * D).rearrange("p (t d) -> p t d", d=D) for _ in range(2)]
        assert at[0] == SLOTS * COLS * D
        wq_s, wk_s, wv_s = (part(NT * D).rearrange("p (t d) -> p t d", d=D) for _ in range(3))
        we_s = part(ET * D).rearrange("p (e d) -> p e d", d=D)
        w0T = part(2 * D).rearrange("p (a d) -> p a d", d=D)
        w0_s = part(2 * D)
        kT = [part(P) for _ in range(2)]
        tmp0 = part(CW)
        tmp1 = part(CW)

        bank = [ps(f"bank{i}", [P, 2, 512]) for i in range(4)]
        flat = [b[:, :, :].rearrange("p a b -> p (a b)") for b in bank]

        psKQV = [bank[0][:, 0, :], bank[0][:, 1, :], bank[1][:, 0, :], bank[1][:, 1, :]]

        L = {n: sem("loaded_" + n) for n in ("src", "dst", "etype", "x", "weights", "small", "x1")}
        gates_passed = sem("gates_passed")
        consts_ready = sem("consts_ready")
        pool_step = sem("pool_step")
        pads_ready = sem("pads_ready")
        iota_ready = sem("iota_ready")
        setup_vec = sem("setup_vec")
        dst_ready = sem("dst_ready")
        first_ps = sem("first_ps")
        inside_ready = sem("inside_ready")
        inside_ps = sem("inside_ps")
        passes_ready = sem("passes_ready")
        w0_ps = sem("w0_ps")
        w0_ready = sem("w0_ready")
        x_copied = sem("x_copied")
        xT_ps = sem("xT_ps")
        xT_ready = sem("xT_ready")
        sums_zero = sem("sums_zero")
        l0_tables = sem("l0_tables")
        l0_idx = sem("l0_idx")
        l0_rows = [sem(f"l0_rows{u}") for u in range(SLOTS)]
        l0_free = [sem(f"l0_free{u}") for u in range(SLOTS)]
        l0_hot = sem("l0_hot")
        l0_hot_used = sem("l0_hot_used")
        l0_part = sem("l0_part")
        l0_vec = sem("l0_vec")
        mean_ready = sem("mean_ready")
        denseT_ps = sem("denseT_ps")
        relu_ready = sem("relu_ready")
        dense_ps = sem("dense_ps")
        var_ready = sem("var_ready")
        std_ready = sem("std_ready")
        x1_ready = sem("x1_ready")
        x1_stored = sem("x1_stored")
        a_vec = sem("a_vec")
        typed_ready = sem("typed_ready")
        typedT_ps = sem("typedT_ps")
        typedT_ready = sem("typedT_ready")
        k_ps = sem("k_ps")
        q_ps = sem("q_ps")
        v_ps = sem("v_ps")
        kT_ready = sem("kT_ready")
        kw_ps = sem("kw_ps")
        kw_low = sem("kw_low")
        kw_high = sem("kw_high")
        v_rows = sem("v_rows")
        row_stored = [sem(f"row_stored{k}") for k in range(2)]
        l1_start = sem("l1_start")
        l1_tables = sem("l1_tables")
        l1_idx = sem("l1_idx")
        l1_pass = sem("l1_pass")
        l1_rows = [sem(f"l1_rows{u}") for u in range(SLOTS)]
        l1_free = [sem(f"l1_free{u}") for u in range(SLOTS)]
        away_ready = sem("away_ready")
        keysT_ps = sem("keysT_ps")
        keysT_ready = sem("keysT_ready")
        score_ps = sem("score_ps")
        max_ready = sem("max_ready")
        prob_ready = sem("prob_ready")
        probT_ps = sem("probT_ps")
        prob_copied = sem("prob_copied")
        spread_ready = sem("spread_ready")
        rep_ps = sem("rep_ps")
        part_ps = sem("part_ps")
        delta_ready = sem("delta_ready")
        factor_ready = sem("factor_ready")
        l1_vec = sem("l1_vec")
        l1_done = sem("l1_done")
        attn_ready = sem("attn_ready")
        attn_ps = sem("attn_ps")
        c_var = sem("c_var")
        c_std = sem("c_std")
        c_vec = sem("c_vec")
        y_ready = sem("y_ready")
        stored = sem("stored")

        block = ctx.enter_context(nc.Block())

        def gate(e, s, value):
            e.wait_ge(s, value)
            e.sem_inc(gates_passed, 1)

        def blocks(e, ps_, body):
            with e.Fori(0, NBLK // SLOTS) as i:
                for u in range(SLOTS):
                    body(ps_ * NBLK + i * SLOTS + u, i * SLOTS + u, u, ps_ * TURNS[u] + i)
            for u in range(NBLK % SLOTS):
                b = NBLK - NBLK % SLOTS + u
                body(ps_ * NBLK + b, b, u, ps_ * TURNS[u] + b // SLOTS)

        def passes(e):
            e.wait_ge(passes_ready, 1)
            return e.value_load(passes_i[0:1, 0:1], min_val=1, max_val=NPASS)

        def load_edges(e, tile, dram, s):
            e.dma_start(tile[:, 0:FULL * RUN].rearrange("p (h j) -> p h j", j=RUN),
                        dram[0:FULL * HALF].rearrange("(h p j) -> p h j", p=P, j=RUN)).then_inc(s, 16)
            e.dma_start(tile[0:REST // RUN, FULL * RUN:NHALF * RUN],
                        dram[FULL * HALF:E].rearrange("(p j) -> p j", j=RUN)).then_inc(s, 16)

        def wait_row_free(e, n, k):
            e.wait_ge(row_stored[k], (n - k) * 8 + 16)

        @block.sync
        def _(sp):
            sp.wait_ge(pads_ready, 3)
            load_edges(sp, dst_i, dst, L["dst"])
            load_edges(sp, src_idx[:, :].bitcast(I32), src, L["src"])
            load_edges(sp, etype_i, etype, L["etype"])
            sp.wait_ge(pads_ready, 4)
            sp.dma_start(x_nodes[:, 0:TILES - 1, :],
                         x[0:(TILES - 1) * P, :].rearrange("(t p) d -> p t d", p=P)).then_inc(L["x"], 16)
            sp.dma_start(x_nodes[0:LAST, TILES - 1, :], x[(TILES - 1) * P:N, :]).then_inc(L["x"], 16)
            sp.dma_start(w0_s, w0[:, :]).then_inc(L["weights"], 16)
            for w_s, w in ((wq_s, wq), (wk_s, wk), (wv_s, wv), (we_s, we)):
                sp.dma_start(w_s, w.rearrange("t i o -> i t o")).then_inc(L["weights"], 16)
            with sp.Fori(0, CHUNKS) as c:
                sp.wait_ge(x1_ready, c + 1)
                sp.dma_start(x1_view[:, bass.ds(c * CH, CH), :], x_nodes[:, bass.ds(c * CH, CH), :]).then_inc(x1_stored, 16)

            for k in range(2):
                sp.sem_inc(row_stored[k], 16)

            def store_rows(n, k):
                gate(sp, kw_low, n + 1)
                gate(sp, kw_high, n + 1)
                gate(sp, v_rows, n + 2)
                sp.dma_start(table_tiles[bass.ds(n * P, P), :], kv_rows[k].rearrange("p e c -> p (e c)")).then_inc(row_stored[k], 16)

            with sp.Fori(0, TILES // 2) as i:
                for k in range(2):
                    store_rows(i * 2 + k, k)
            store_rows(TILES - 1, 0)
            sp.wait_ge(l1_done, 1)
            sp.dma_start(x_nodes, x1_view).then_inc(L["x1"], 16)
            o_full = out[0:(TILES - 1) * P, :].rearrange("(t p) d -> p t d", p=P)
            with sp.Fori(0, CHUNKS - 1) as c:
                sp.wait_ge(y_ready, c + 1)
                sp.dma_start(o_full[:, bass.ds(c * CH, CH), :], x_nodes[:, bass.ds(c * CH, CH), :]).then_inc(stored, 16)
            sp.wait_ge(y_ready, CHUNKS)
            sp.dma_start(o_full[:, TILES - CH:TILES - 1, :], x_nodes[:, TILES - CH:TILES - 1, :]).then_inc(stored, 16)
            sp.dma_start(out[(TILES - 1) * P:N, :], x_nodes[0:LAST, TILES - 1, :]).then_inc(stored, 16)
            sp.wait_ge(stored, 16 * (CHUNKS + 1))

        @block.gpsimd
        def _(pool):
            tail = slice(FULL * RUN, NHALF * RUN)
            pool.memset(dst_i[:, tail], -4096).then_inc(pads_ready, 1)
            pool.memset(src_idx[:, tail], 0).then_inc(pads_ready, 1)
            pool.memset(etype_i[:, tail], 0).then_inc(pads_ready, 1)
            pool.memset(nodes[:, NPAD - P:NACC], 0.0).then_inc(pads_ready, 1)
            pool.iota(iota_i[:, :], pattern=[[1, WIN]], base=0, channel_multiplier=0).then_inc(iota_ready, 1)
            pool.memset(identf[:, :], 0.0).then_inc(pool_step, 1)
            pool.wait_ge(pool_step, 1)
            pool.affine_select(out=identf[:, :], in_=identf[:, :], compare_op=ALU.not_equal, fill=1.0, base=0,
                               pattern=[[-1, P]], channel_multiplier=1).then_inc(consts_ready, 1)
            pool.memset(onesf[:, :], 1.0).then_inc(consts_ready, 1)
            pool.memset(eps_col[:, :], LN_EPS).then_inc(consts_ready, 1)
            pool.dma_start(ntype_i[:, 0:TILES - 1], ntype[0:(TILES - 1) * P].rearrange("(t p) -> p t", p=P),
                           allow_slow_non_contiguous=True).then_inc(L["small"], 16)
            pool.dma_start(ntype_i[0:LAST, TILES - 1:TILES], ntype[(TILES - 1) * P:N].rearrange("(p t) -> p t", t=1)
                           ).then_inc(L["small"], 16)
            pool.dma_start(bias_c[:, :], b0.rearrange("(d a) -> d a", a=1)).then_inc(L["small"], 16)
            pool.dma_start(mu_b[:, :], mu.rearrange("(a d) -> a d", a=1).broadcast_to([P, ET])).then_inc(L["small"], 16)
            count = passes(pool)

            def gather(rows, table_, idx, rows_sem, free_sem, idx_sem):
                def body(it, b, u, turn):
                    gate(pool, free_sem[u], turn + 1)
                    pool.tensor_copy(stage[:, u, :], idx[:, bass.ds(b * COLS, COLS)]).then_inc(idx_sem, 1)
                    gate(pool, idx_sem, it + 1)
                    for j in range(COLS):
                        pool.indirect_dma_start(rows[u][:, j, :], None, table_,
                                                bass.IndirectOffsetOnAxis(ap=stage[:, u, j:j + 1], axis=0)
                                                ).then_inc(rows_sem[u], 16)
                return body

            pool.wait_ge(L["src"], 32)
            with pool.Fori(0, count) as ps_:
                blocks(pool, ps_, gather(x_ring, x, src_idx, l0_rows, l0_free, l0_idx))
            pool.wait_ge(row_stored[0], 16 * (-(-TILES // 2)) + 16)
            pool.wait_ge(row_stored[1], 16 * (TILES // 2) + 16)
            with pool.Fori(0, count) as ps_:
                blocks(pool, ps_, gather(kv_ring, table, key_idx, l1_rows, l1_free, l1_idx))

        @block.tensor
        def _(pe):
            pe.wait_ge(consts_ready, 3)
            pe.wait_ge(dst_ready, 1)
            pe.matmul(flat[0][:, 0:NHALF], onesf[0:1, :],
                      dst_f[0:1, :].rearrange("p (h j) -> p h j", j=RUN)[:, :, 0], start=True, stop=True
                      ).then_inc(first_ps, 1)
            pe.wait_ge(inside_ready, 1)
            pe.matmul(flat[1][:, 0:1], onesf[:, :], step_f[:, 0:1], start=True, stop=True).then_inc(inside_ps, 1)
            pe.wait_ge(L["weights"], 80)
            pe.transpose(flat[2][:, 0:P], w0_s[:, 0:D], identf[:, :])
            pe.transpose(flat[2][:, P:2 * P], w0_s[:, D:2 * D], identf[:, :]).then_inc(w0_ps, 1)
            pe.wait_ge(L["x"], 32)
            with pe.Fori(0, CHUNKS) as c:
                pe.wait_ge(x_copied, c + 1)
                for t in range(CH):
                    tr = pe.transpose(flat[3][:, t * P:(t + 1) * P], tmp0[:, t * P:(t + 1) * P], identf[:, :])
                tr.then_inc(xT_ps, 1)
            count = passes(pe)
            def l0_block(it, b, u, turn):
                pe.wait_ge(l0_hot, it + 1)
                pe.wait_ge(l0_rows[u], (turn + 1) * (16 * COLS))
                for h in range(2):
                    for what in range(2):
                        for j in range(RUN):
                            o = (h * 2 + what) * WIN
                            mm = pe.matmul(flat[0][:, o:o + WIN],
                                           onesf[:, :] if what else x_ring[u][:, h * RUN + j, :],
                                           hot[:, h * RUN + j, :], start=(j == 0), stop=(j == RUN - 1))
                mm.then_inc(l0_part, 1)

            with pe.Fori(0, count) as ps_:
                blocks(pe, ps_, l0_block)

            pe.wait_ge(w0_ready, 1)
            with pe.Fori(0, CHUNKS) as c:
                pe.wait_ge(mean_ready, c + 1)
                for a in range(2):
                    part_cols = bass.ds(c * CW + a * (CW // 2), CW // 2)
                    psH = bank[3][:, a, 0:CW // 2]
                    pe.matmul(psH, w0T[:, 0, :], negmax[:, part_cols], start=True, stop=False)
                    mm = pe.matmul(psH, w0T[:, 1, :], sums[:, 0, part_cols], start=False, stop=True)
                mm.then_inc(denseT_ps, 1)
                pe.wait_ge(relu_ready, c + 1)
                for t in range(CH):
                    tr = pe.transpose(flat[2][:, t * P:(t + 1) * P], tmp0[:, t * P:(t + 1) * P], identf[:, :])
                tr.then_inc(dense_ps, 1)

            def project(n, k):
                psX, psK, psQ, psV, psW = *psKQV, flat[2 + k]
                pe.wait_ge(typed_ready, n + 1)
                for t in range(NT):
                    tr = pe.transpose(psX[:, t * P:(t + 1) * P], x1_typed[k][:, t, :], identf[:, :])
                tr.then_inc(typedT_ps, 1)
                pe.wait_ge(typedT_ready, n + 1)
                for t in range(NT):
                    mm = pe.matmul(psK[:, 0:P], wk_s[:, t, :], x1_typedT[k][:, t, :], start=(t == 0), stop=(t == NT - 1))
                mm.then_inc(k_ps, 1)
                pe.wait_ge(v_rows, n + 1)
                for t in range(NT):
                    mm = pe.matmul(psQ[:, 0:P], wq_s[:, t, :], x1_typedT[k][:, t, :], start=(t == 0), stop=(t == NT - 1))
                mm.then_inc(q_ps, 1)
                for t in range(NT):
                    mm = pe.matmul(psV[:, 0:P], x1_typedT[k][:, t, :], wv_s[:, t, :], start=(t == 0), stop=(t == NT - 1))
                mm.then_inc(v_ps, 1)
                pe.wait_ge(kT_ready, n + 1)
                for a in range(2):
                    mm = pe.matmul(psW[:, a * 512:(a + 1) * 512], kT[k], we_s[:, a * 4:a * 4 + 4, :], start=True, stop=True)
                mm.then_inc(kw_ps, 1)

            with pe.Fori(0, TILES // 2) as i:
                for k in range(2):
                    project(i * 2 + k, k)
            project(TILES - 1, 0)

            psT = [bank[0][:, 0, :], bank[0][:, 1, :]]
            psS, psP = flat[1], flat[2]
            psA, psR = bank[3][:, 0, :], bank[3][:, 1, :]

            def l1_block(it, b, u, turn):
                pe.wait_ge(away_ready, it + 1)
                for h in range(2):
                    for q in range(2):
                        for j in range(4):
                            mm = pe.matmul(psS[h * WIN:(h + 1) * WIN, q * 512 + j * P:q * 512 + (j + 1) * P],
                                           away[:, h * RUN + q * 4 + j, :], negid[:, :],
                                           start=(j == 0), stop=False, skip_group_check=True)
                pe.wait_ge(l1_rows[u], (turn + 1) * (16 * COLS))
                for g in range(4):
                    h, q = g // 2, g % 2
                    if g >= 2:
                        pe.wait_ge(keysT_ready, it * 4 + g - 1)
                    for j in range(4):
                        tr = pe.transpose(psT[g % 2][:, j * P:(j + 1) * P], kv_ring[u][:, g * 4 + j, 0:D], identf[:, :])
                    tr.then_inc(keysT_ps, 1)
                for g in range(4):
                    h, q = g // 2, g % 2
                    pe.wait_ge(keysT_ready, it * 4 + g + 1)
                    mm = pe.matmul(psS[h * WIN:(h + 1) * WIN, q * 512:(q + 1) * 512], queries[:, h, :],
                                   keysT[:, g, :], start=False, stop=True, skip_group_check=True)
                mm.then_inc(score_ps, 1)
                pe.wait_ge(prob_ready, it + 1)
                for j in range(RUN):
                    tr = pe.transpose(psP[:, j * P:(j + 1) * P], probT[:, j * P:(j + 1) * P], identf[:, :])
                tr.then_inc(probT_ps, 1)
                pe.wait_ge(spread_ready, it + 1)
                pe.matmul(psR[:, 0:P], onesf[:, :], spread[:, 0, :], start=True, stop=True).then_inc(rep_ps, 1)
                for h in range(2):
                    pe.matmul(psA[:, (2 * h + 1) * WIN:(2 * h + 2) * WIN], onesf[:, :],
                              spread[:, 1, h * WIN:(h + 1) * WIN], start=True, stop=True)
                pe.wait_ge(prob_copied, it + 1)
                for h in range(2):
                    for j in range(RUN):
                        mm = pe.matmul(psA[:, 2 * h * WIN:(2 * h + 1) * WIN], kv_ring[u][:, h * RUN + j, D:2 * D],
                                       prob[:, j, h * WIN:(h + 1) * WIN], start=(j == 0), stop=(j == RUN - 1))
                mm.then_inc(part_ps, 1)

            pe.wait_ge(l1_start, 1)
            with pe.Fori(0, count) as ps_:
                gate(pe, l1_pass, ps_ + 1)
                blocks(pe, ps_, l1_block)
            pe.drain().then_inc(l1_done, 1)

            with pe.Fori(0, CHUNKS) as c:
                pe.wait_ge(attn_ready, c + 1)
                for t in range(CH):
                    tr = pe.transpose(flat[0][:, t * P:(t + 1) * P], tmp0[:, t * P:(t + 1) * P], identf[:, :])
                tr.then_inc(attn_ps, 1)

        @block.scalar
        def _(act):
            act.wait_ge(w0_ps, 1)
            act.activation(w0T[:, :, :], flat[2][:, 0:2 * P].rearrange("p (a d) -> p a d", d=D), ACT.Copy).then_inc(w0_ready, 1)
            act.wait_ge(L["x"], 32)
            with act.Fori(0, CHUNKS) as c:
                act.activation(tmp0, nodes[:, bass.ds(c * CW, CW)], ACT.Copy).then_inc(x_copied, 1)
                act.wait_ge(xT_ps, c + 1)
                act.activation(negmax[:, bass.ds(c * CW, CW)], flat[3][:, 0:CW], ACT.Copy).then_inc(xT_ready, 1)
            act.wait_ge(L["small"], 64)
            with act.Fori(0, CHUNKS) as c:
                act.wait_ge(denseT_ps, c + 1)
                act.activation(tmp0.rearrange("p (a n) -> p a n", a=2), bank[3][:, :, 0:CW // 2], ACT.Relu,
                               bias=bias_c[:, 0:1]).then_inc(relu_ready, 1)
                act.wait_ge(var_ready, c + 1)
                act.activation(std[:, :], aggr[:, :, 1], ACT.Sqrt, bias=eps_col[:, 0:1]).then_inc(std_ready, 1)

            def project(n, k):
                _, psK, psQ, psV, psW = *psKQV, flat[2 + k]
                act.wait_ge(k_ps, n + 1)
                act.activation(kT[k], psK[:, 0:P], ACT.Copy).then_inc(kT_ready, 1)
                act.wait_ge(q_ps, n + 1)
                act.activation(nodes[:, bass.ds(n * P, P)], psQ[:, 0:P], ACT.Copy)
                act.wait_ge(v_ps, n + 1)
                wait_row_free(act, n, k)
                act.activation(kv_rows[k][:, :, D:2 * D], psV[:, 0:P].unsqueeze(1).broadcast_to([P, ET, D]),
                               ACT.Copy).then_inc(v_rows, 1)
                act.wait_ge(kw_ps, n + 1)
                act.activation(kv_rows[k][:, 4:8, 0:D], psW[:, 512:1024].rearrange("p (e d) -> p e d", d=D),
                               ACT.Copy).then_inc(kw_high, 1)

            act.sem_inc(v_rows, 1)
            act.wait_ge(x1_stored, 16 * CHUNKS)
            with act.Fori(0, TILES // 2) as i:
                for k in range(2):
                    project(i * 2 + k, k)
            project(TILES - 1, 0)
            act.drain().then_inc(l1_start, 1)
            act.wait_ge(l1_start, 1)
            count = passes(act)
            psT = [bank[0][:, 0, :], bank[0][:, 1, :]]

            def l1_block(it, b, u, turn):
                for g in range(4):
                    act.wait_ge(keysT_ps, it * 4 + g + 1)
                    act.activation(keysT[:, g, :], psT[g % 2], ACT.Copy).then_inc(keysT_ready, 1)
                act.wait_ge(max_ready, it + 1)
                act.activation(probT[:, :], flat[1], ACT.Exp, bias=cols[:, 1:2], accum_out=cols[:, 2:3]
                               ).then_inc(prob_ready, 1)
                for h in range(2):
                    act.wait_ge(delta_ready, it * 2 + h + 1)
                    act.activation(factor[:, :, :], delta[:, :, :], ACT.Exp).then_inc(factor_ready, 1)

            with act.Fori(0, count) as ps_:
                blocks(act, ps_, l1_block)
            with act.Fori(0, CHUNKS) as c:
                act.wait_ge(c_var, c + 1)
                act.activation(std[:, :], aggr[:, :, 1], ACT.Sqrt, bias=eps_col[:, 0:1]).then_inc(c_std, 1)

        @block.vector
        def _(dve):
            steps = [0]

            def setup(ins):
                steps[0] += 1
                ins.then_inc(setup_vec, 1)
                dve.wait_ge(setup_vec, steps[0])

            dve.wait_ge(L["dst"], 32)
            setup(dve.tensor_copy(dst_f[:, :], dst_i))
            dve.sem_inc(dst_ready, 1)
            dve.wait_ge(consts_ready, 3)
            dve.wait_ge(iota_ready, 1)
            dve.tensor_copy(iota_f[:, :], iota_i[:, :])
            dve.tensor_copy(identb[:, :], identf[:, :])
            dve.tensor_scalar(negid[:, :], identf[:, :], NEG, None, ALU.mult)
            dve.wait_ge(first_ps, 1)
            setup(dve.tensor_copy(first[:, :], flat[0][:, 0:NHALF]))
            edges = lambda t: t[:, :].rearrange("p (h j) -> p h j", j=RUN)
            over = lambda t: t[:, :].unsqueeze(2).broadcast_to([P, NHALF, RUN])
            setup(dve.tensor_tensor(edges(rel), edges(dst_f), over(first), ALU.subtract))
            wide = ring[:, 0:NHALF * RUN]
            setup(dve.tensor_scalar(wide, rel[:, :], float(WIN), None, ALU.is_lt))
            setup(dve.scalar_tensor_tensor(wide, rel[:, :], 0.0, wide, ALU.is_ge, ALU.mult))
            setup(dve.reduce_sum(step_f[:, 0:1], wide, AX))
            dve.sem_inc(inside_ready, 1)
            dve.wait_ge(inside_ps, 1)
            setup(dve.tensor_scalar(step_f[:, 1:2], flat[1][:, 0:1], float(E), None, ALU.is_equal))
            setup(dve.tensor_scalar(step_f[:, 2:3], step_f[:, 1:2], -float(WIN), float(WIN), ALU.mult, ALU.add))
            setup(dve.tensor_scalar(passes_i[0:1, 0:1], step_f[0:1, 1:2], float(1 - NPASS), float(NPASS), ALU.mult, ALU.add))
            dve.sem_inc(passes_ready, 1)
            setup(dve.memset(sums[:, :, :], 0.0))
            count = passes(dve)

            def tables(chain, ps_):
                def link(ins, k):
                    ins.then_inc(chain, 1)
                    dve.wait_ge(chain, ps_ * 3 + k)
                link(dve.scalar_tensor_tensor(base_f[:, :], first[:, :], step_f[:, 1:2],
                                              step_f[:, 3:4].broadcast_to([P, NHALF]), ALU.mult, ALU.add), 1)
                dve.tensor_scalar(step_f[:, 3:4], step_f[:, 3:4], step_f[:, 2:3], None, ALU.add).then_inc(chain, 1)
                dve.tensor_copy(base_i[0:1, :], base_f[0:1, :])
                dve.tensor_tensor(edges(rel), edges(dst_f), over(base_f), ALU.subtract).then_inc(chain, 1)
                gate(dve, chain, ps_ * 3 + 3)

            def member(out_, b, op):
                return dve.tensor_tensor(
                    out_, rel[:, bass.ds(b * COLS, COLS)].unsqueeze(2).broadcast_to([P, COLS, WIN]),
                    iota_f[:, :].unsqueeze(1).broadcast_to([P, COLS, WIN]), op)

            def l0_block(it, b, u, turn):
                base = [dve.value_load(base_i[0:1, bass.ds(b * 2 + h, 1)], min_val=0, max_val=N - 1) for h in range(2)]
                member(hot, b, ALU.is_equal).then_inc(l0_hot, 1)
                dve.wait_ge(l0_part, it + 1)
                dve.sem_inc(l0_free[u], 1)
                for h in range(2):
                    dve.wait_ge(l0_vec, it * 2 + h + 1)
                    win = sums[:, :, bass.ds(base[h], WIN)]
                    dve.tensor_tensor(win, flat[0][:, h * 2 * WIN:(h + 1) * 2 * WIN].rearrange("p (a w) -> p a w", w=WIN),
                                      win, ALU.add).then_inc(l0_vec, 1)

            setup(dve.memset(step_f[:, 3:4], 0.0))
            dve.sem_inc(l0_vec, 1)
            for u in range(SLOTS):
                dve.sem_inc(l0_free[u], 1)
            with dve.Fori(0, count) as ps_:
                tables(l0_tables, ps_)
                blocks(dve, ps_, l0_block)

            dve.wait_ge(L["etype"], 32)
            dve.wait_ge(L["src"], 32)
            dve.wait_ge(L["small"], 64)
            dve.scalar_tensor_tensor(key_idx[:, :], src_idx[:, :].bitcast(I32), float(ET), etype_i, ALU.mult, ALU.add)
            for t in range(NT):
                dve.tensor_scalar(ntype_m[:, 0:TILES - 1, t], ntype_i[:, 0:TILES - 1], float(t), None, ALU.is_equal)
            setup(dve.memset(ntype_m[:, TILES - 1, :], 0.0))
            for t in range(NT):
                dve.tensor_scalar(ntype_m[0:LAST, TILES - 1, t:t + 1], ntype_i[0:LAST, TILES - 1:TILES], float(t), None,
                                  ALU.is_equal)
            dve.wait_ge(L["weights"], 80)
            for e in range(ET):
                ins = dve.tensor_scalar(we_s[:, e, :], we_s[:, e, :], mu_b[:, e:e + 1], SCALE, ALU.mult, ALU.mult)
            setup(ins)
            dve.wait_ge(xT_ready, CHUNKS)


            def norm(chain, c0, v_sem, s_sem, c, src_tile):
                for t in range(CH):
                    ins = dve.bn_stats(stats[:, t, :], src_tile[:, t * P:(t + 1) * P])
                ins.then_inc(chain, 1)
                gate(dve, chain, c0 + 1)
                for t in range(CH):
                    ins = dve.bn_aggr(aggr[:, t, :], stats[:, t, :])
                ins.then_inc(v_sem, 1)
                dve.wait_ge(s_sem, c + 1)
                dve.reciprocal(std[:, :], std[:, :]).then_inc(chain, 1)
                dve.wait_ge(chain, c0 + 2)
                for t in range(CH):
                    ins = dve.tensor_scalar(nodes[:, bass.ds(c * CW + t * P, P)], src_tile[:, t * P:(t + 1) * P],
                                            aggr[:, t, 0:1], std[:, t:t + 1], ALU.subtract, ALU.mult)
                return ins

            with dve.Fori(0, CHUNKS) as c:
                w = bass.ds(c * CW, CW)
                K = 6

                def link(ins, k):
                    ins.then_inc(a_vec, 1)
                    dve.wait_ge(a_vec, c * K + k)
                link(dve.tensor_scalar(tmp0, sums[:, 1, w], 1.0, None, ALU.max), 1)
                link(dve.reciprocal(tmp0, tmp0), 2)
                dve.scalar_tensor_tensor(tmp1, sums[:, 1, w], 0.0, negmax[:, w], ALU.is_equal, ALU.mult)
                link(dve.tensor_tensor(sums[:, 0, w], sums[:, 0, w], tmp0, ALU.mult), 3)
                dve.tensor_tensor(sums[:, 0, w], sums[:, 0, w], tmp1, ALU.add).then_inc(mean_ready, 1)
                dve.wait_ge(dense_ps, c + 1)
                link(dve.tensor_tensor(tmp1, flat[2][:, 0:CW], nodes[:, w], ALU.add), 4)
                norm(a_vec, c * K + 4, var_ready, std_ready, c, tmp1).then_inc(x1_ready, 1)

            def project(n, k):
                rows = nodes[:, bass.ds(n * P, P)]
                for t in range(NT):
                    m = ntype_m[:, bass.ds(n, 1), t:t + 1].rearrange("p a b -> p (a b)")
                    ins = dve.tensor_scalar(x1_typed[k][:, t, :], rows, m, None, ALU.mult)
                ins.then_inc(typed_ready, 1)
                dve.wait_ge(typedT_ps, n + 1)
                dve.tensor_copy(x1_typedT[k].rearrange("p t d -> p (t d)"), psKQV[0]).then_inc(typedT_ready, 1)
                dve.wait_ge(kw_ps, n + 1)
                wait_row_free(dve, n, k)
                dve.tensor_copy(kv_rows[k][:, 0:4, 0:D], flat[2 + k][:, 0:512].rearrange("p (e d) -> p e d", d=D)
                                ).then_inc(kw_low, 1)

            with dve.Fori(0, TILES // 2) as i:
                for k in range(2):
                    project(i * 2 + k, k)
            project(TILES - 1, 0)

            setup(dve.memset(sums[:, :, :], 0.0))
            setup(dve.memset(negmax[:, :], -FLOOR))
            setup(dve.memset(step_f[:, 3:4], 0.0))
            dve.wait_ge(l1_start, 1)
            for u in range(SLOTS):
                dve.sem_inc(l1_free[u], 1)
            psS, psP = flat[1], flat[2]
            psA, psR = bank[3][:, 0, :], bank[3][:, 1, :]

            def l1_block(it, b, u, turn):
                base = [dve.value_load(base_i[0:1, bass.ds(b * 2 + h, 1)], min_val=0, max_val=N - 1) for h in range(2)]
                K = 9
                k = [0]

                def link(ins):
                    k[0] += 1
                    ins.then_inc(l1_vec, 1)
                    dve.wait_ge(l1_vec, it * K + k[0])
                for h in range(2):
                    dve.tensor_copy(queries[:, h, :], nodes[:, bass.ds(base[h], WIN)])
                member(away[:, :, :], b, ALU.not_equal).then_inc(away_ready, 1)
                dve.wait_ge(score_ps, it + 1)
                link(dve.reduce_max(cols[:, 0:1], psS, AX))
                dve.tensor_scalar(cols[:, 1:2], cols[:, 0:1], FLOOR, -1.0, ALU.max, ALU.mult).then_inc(max_ready, 1)
                dve.wait_ge(max_ready, it + 1)
                dve.tensor_scalar(spread[:, 0, :], identf[:, :], cols[:, 1:2], None, ALU.mult)
                dve.wait_ge(prob_ready, it + 1)
                dve.tensor_scalar(spread[:, 1, :], identf[:, :], cols[:, 2:3], None, ALU.mult).then_inc(spread_ready, 1)
                dve.wait_ge(probT_ps, it + 1)
                dve.tensor_copy(prob[:, :, :].rearrange("p a b -> p (a b)"), psP).then_inc(prob_copied, 1)
                dve.wait_ge(rep_ps, it + 1)
                for h in range(2):
                    win = bass.ds(base[h], WIN)
                    new = psR[:, h * WIN:(h + 1) * WIN]
                    link(dve.tensor_tensor(scaled[:, 0, 0, :], new, negmax[:, win], ALU.min))
                    dve.tensor_tensor(delta[:, 0, :], scaled[:, 0, 0, :], negmax[:, win], ALU.subtract)
                    dve.tensor_tensor(delta[:, 1, :], scaled[:, 0, 0, :], new, ALU.subtract).then_inc(delta_ready, 1)
                    gate(dve, delta_ready, it * 2 + h + 1)
                    link(dve.tensor_copy(negmax[:, win], scaled[:, 0, 0, :]))
                    dve.wait_ge(factor_ready, it * 2 + h + 1)
                    dve.tensor_tensor(scaled[:, 0, :, :], sums[:, :, win],
                                      factor[:, 0, :].unsqueeze(1).broadcast_to([P, 2, WIN]), ALU.mult)
                    if h == 0:
                        dve.wait_ge(part_ps, it + 1)
                        dve.sem_inc(l1_free[u], 1)
                    link(dve.tensor_tensor(scaled[:, 1, :, :],
                                           psA[:, h * 2 * WIN:(h + 1) * 2 * WIN].rearrange("p (a w) -> p a w", w=WIN),
                                           factor[:, 1, :].unsqueeze(1).broadcast_to([P, 2, WIN]), ALU.mult))
                    link(dve.tensor_tensor(sums[:, :, win], scaled[:, 0, :, :], scaled[:, 1, :, :], ALU.add))
                assert k[0] == K
                dve.sem_inc(gates_passed, 1)

            with dve.Fori(0, count) as ps_:
                tables(l1_tables, ps_)
                dve.sem_inc(l1_pass, 1)
                blocks(dve, ps_, l1_block)

            dve.wait_ge(L["x1"], 16)
            with dve.Fori(0, CHUNKS) as c:
                w = bass.ds(c * CW, CW)
                K = 5

                def link(ins, k):
                    ins.then_inc(c_vec, 1)
                    dve.wait_ge(c_vec, c * K + k)
                link(dve.tensor_scalar(tmp0, sums[:, 1, w], SUM_EPS, None, ALU.add), 1)
                link(dve.reciprocal(tmp0, tmp0), 2)
                dve.tensor_tensor(tmp0, sums[:, 0, w], tmp0, ALU.mult).then_inc(attn_ready, 1)
                dve.wait_ge(attn_ps, c + 1)
                link(dve.tensor_tensor(tmp1, flat[0][:, 0:CW], nodes[:, w], ALU.add), 3)
                norm(c_vec, c * K + 3, c_var, c_std, c, tmp1).then_inc(y_ready, 1)


_INS = ["x", "src", "dst", "edge_type_8", "node_type_4", "L0_gnn_W", "L0_gnn_b", "L1_gnn_W_Q", "L1_gnn_W_K",
        "L1_gnn_W_V", "L1_gnn_W_edge", "L1_gnn_mu"]


def kernel(**inputs):
    import numpy as _np
    import concourse.bacc as _bacc
    from concourse import mybir as _mybir
    from concourse.bass_utils import run_bass_kernel_spmd as _run

    nc = _bacc.Bacc("TRN2", target_bir_lowering=False, num_devices=1)
    arrays, args = {}, []
    for name in _INS:
        a = _np.ascontiguousarray(inputs[name])
        arrays[f"in_{name}_dram"] = a
        args.append(nc.dram_tensor(f"in_{name}_dram", a.shape, _mybir.dt.from_np(a.dtype), kind="ExternalInput").ap())
    args.append(nc.dram_tensor("out_0_dram", inputs["x"].shape, _mybir.dt.float32, kind="ExternalOutput").ap())
    gnn_kernel(nc, *args)
    r = _run(nc, [arrays], core_ids=[0])
    return r.results[0]["out_0_dram"]
```

```python
from collections import namedtuple
from contextlib import ExitStack

import concourse.bass as bass
from concourse import mybir

ALU = mybir.AluOpType
ACT = mybir.ActivationFunctionType
AX = mybir.AxisListType.X
F32 = mybir.dt.float32
BF16 = mybir.dt.bfloat16
I32 = mybir.dt.int32
U32 = mybir.dt.uint32

P = 128
RUN = 8
HALF = P * RUN
BLOCK = 2 * HALF
COLS = 2 * RUN
WIN = 64
SLOTS0 = 4
SLOTS1 = 3
NEG = -1.0e30
FLOOR = -1.0e9
LN_EPS = 1e-5
SUM_EPS = 1e-10

Pair = namedtuple("Pair", "it b v turn")
Block = namedtuple("Block", "it b u turn")
Tile = namedtuple("Tile", "n t k turn")


def gnn_kernel(nc, x, src, dst, etype, ntype, w0, b0, wq, wk, wv, we, mu, out):
    N, D = x.shape
    E = src.shape[0]
    NT = wq.shape[0]
    ET = we.shape[0]
    assert D == P and NT * D == 512 and ET * D == 1024
    TILES = -(-N // P)
    LAST = N - (TILES - 1) * P
    NPAD = TILES * P
    CH = 7
    CHUNKS = TILES // CH
    CW = CH * P
    assert CHUNKS * CH == TILES
    NBLK = -(-E // BLOCK)
    NHALF = 2 * NBLK
    EDGE_COLS = NHALF * RUN
    FULL = E // HALF
    REST = E - FULL * HALF
    assert FULL == NHALF - 1 and REST % RUN == 0 and REST > 0
    assert NBLK == 2 * TILES and NBLK % 4 == 2 and NBLK % SLOTS1 == 2
    NPASS = NPAD // WIN + 1
    NACC = NPAD + WIN
    SCALE = float(D) ** -0.5

    with ExitStack() as ctx:
        def sb(name, shape, dt=F32):
            return ctx.enter_context(nc.sbuf_tensor(name, shape, dt))

        def sem(name):
            return ctx.enter_context(nc.semaphore(name))

        table = nc.dram_tensor("kv_table", (NPAD * ET, 2 * D), F32, kind="Internal").ap()
        table_rows = table.rearrange("(n e) c -> n (e c)", e=ET)
        x1_dram = nc.dram_tensor("x1_rows", (NPAD, D), F32, kind="Internal").ap()
        x1_view = x1_dram.rearrange("(t p) d -> p t d", p=P)

        sums = sb("sums", [P, 2, NACC])
        negmax = sb("negmax", [P, NACC])
        queries_all = sb("queries_all", [P, NACC])
        src_idx = sb("src_idx", [P, EDGE_COLS + 2 * COLS], U32)
        key_idx = sb("key_idx", [P, EDGE_COLS + 2 * COLS], U32)
        dst_f = sb("dst_f", [P, EDGE_COLS])
        rel = sb("rel", [P, EDGE_COLS])
        ring = sb("ring", [P, SLOTS1 * COLS * 2 * D])
        stage = sb("stage", [P, 4, COLS], U32)
        keysT = sb("keysT", [P, 4, 512])
        probT = sb("probT", [P, HALF])
        prob = sb("prob", [P, RUN, P])
        away = sb("away", [P, COLS, WIN], BF16)
        identf = sb("identf", [P, P])
        negid = sb("negid", [P, P], BF16)
        onesf = sb("onesf", [P, P])
        onesb = sb("onesb", [P, P], BF16)
        queries = sb("queries", [P, 2, WIN])
        iota_i = sb("iota_i", [P, WIN], I32)
        iota_f = sb("iota_f", [P, WIN])
        bound_i = sb("bound_i", [P, NHALF], I32)
        first = sb("first", [P, NHALF])
        base_f = sb("base_f", [P, NHALF])
        base_i = sb("base_i", [1, NHALF], I32)
        plan = sb("plan", [P, 4])
        passes_i = sb("passes_i", [1, 2], I32)
        cols = sb("cols", [P, 4])
        spread = sb("spread", [P, 2, P])
        larger = sb("larger", [P, WIN])
        delta = sb("delta", [P, 2, WIN])
        factor = sb("factor", [P, 2, WIN])
        scaled = sb("scaled", [P, 2, 2, WIN])
        bias_c = sb("bias_c", [P, 1])
        mu_b = sb("mu_b", [P, ET])
        ntype_i = sb("ntype_i", [P, TILES], I32)
        ntype_m = sb("ntype_m", [P, TILES, NT])
        stats = sb("stats", [P, CH, 6])
        aggr = sb("aggr", [P, 2, CH, 2])
        std = sb("std", [P, 2, CH])
        shift = sb("shift", [P, 2, CH])
        weight = sb("weight", [P, CH])
        eps_col = sb("eps_col", [P, 1])

        dst_i = rel[:, :].bitcast(I32)
        etype_i = keysT[:, :, :].rearrange("p a b -> p (a b)").bitcast(I32)[:, 0:EDGE_COLS]
        flat_keysT = keysT[:, :, :].rearrange("p a b -> p (a b)")
        hot = [probT[:, :].rearrange("p (j w) -> p j w", w=WIN),
               prob[:, :, :].rearrange("p a b -> p (a b)").rearrange("p (j w) -> p j w", w=WIN)]
        hot_b = [away[:, :, :], flat_keysT.bitcast(BF16)[:, 0:COLS * WIN].rearrange("p (j w) -> p j w", w=WIN)]
        x_ring = [ring[:, u * COLS * D:(u + 1) * COLS * D].rearrange("p (j d) -> p j d", d=D) for u in range(SLOTS0)]
        kv_ring = [ring[:, u * COLS * 2 * D:(u + 1) * COLS * 2 * D].rearrange("p (j c) -> p j c", c=2 * D)
                   for u in range(SLOTS1)]
        x1_nodes = queries_all[:, 0:NPAD].rearrange("p (t d) -> p t d", d=D)

        def parts(tile, at, end):
            def part(n):
                at[0] += n
                assert at[0] <= end
                return tile[:, at[0] - n:at[0]]
            return part

        ring_part = parts(ring, [SLOTS0 * COLS * D], SLOTS1 * COLS * 2 * D)
        by_type = lambda t: t.rearrange("p (t d) -> p t d", d=D)
        wq_s, wk_s, wv_s = (by_type(ring_part(NT * D)) for _ in range(3))
        we_s = by_type(ring_part(ET * D))
        w0T = by_type(ring_part(2 * D))
        w0_s = ring_part(2 * D)
        x_tile = [ring_part(D) for _ in range(2)]
        x1_tile = [ring_part(D) for _ in range(2)]
        xT, meanT, reluT, kT = (ring_part(P) for _ in range(4))
        max_part = parts(negmax, [0], NACC)
        kv_rows = [max_part(ET * 2 * D).rearrange("p (e c) -> p e c", c=2 * D) for _ in range(2)]
        x1_typed = by_type(max_part(NT * D))
        x1_typedT = by_type(max_part(NT * D))
        inverse, alone, summed = (max_part(P) for _ in range(3))
        last_part = parts(ring, [0], SLOTS1 * COLS * 2 * D)
        attn, attn_sum, *y_rows = (last_part(CW) for _ in range(4))

        pairs = [ctx.enter_context(nc.psum_tensor(f"banks{i}", [P, 2, 512], F32)) for i in range(4)]
        bank = [pairs[i // 2][:, i % 2, :] for i in range(8)]
        pair = [b[:, :, :].rearrange("p a b -> p (a b)") for b in pairs]

        L = {n: sem("loaded_" + n) for n in ("src", "dst", "etype", "weights", "small", "x1")}
        x_loaded = [sem(f"x_loaded{k}") for k in range(2)]
        gates_passed = sem("gates_passed")
        consts_ready = sem("consts_ready")
        pool_step = sem("pool_step")
        pads_ready = sem("pads_ready")
        setup_vec = sem("setup_vec")
        dst_ready = sem("dst_ready")
        first_ps = sem("first_ps")
        inside_ready = sem("inside_ready")
        inside_ps = sem("inside_ps")
        passes_ready = sem("passes_ready")
        keys_ready = sem("keys_ready")
        w0_ps = sem("w0_ps")
        w0_ready = sem("w0_ready")
        l0_tables = sem("l0_tables")
        l0_idx = sem("l0_idx")
        l0_rows = [sem(f"l0_rows{u}") for u in range(SLOTS0)]
        l0_free = [sem(f"l0_free{u}") for u in range(SLOTS0)]
        hot_ready = sem("hot_ready")
        l0_part = sem("l0_part")
        l0_added = sem("l0_added")
        tile_vec = sem("tile_vec")
        xT_ps = sem("xT_ps")
        xT_copied = sem("xT_copied")
        mean_ready = sem("mean_ready")
        reluT_ps = sem("reluT_ps")
        relu_ready = sem("relu_ready")
        relu_ps = sem("relu_ps")
        var_ready = sem("var_ready")
        std_ready = sem("std_ready")
        x1_ready = sem("x1_ready")
        x1_stored = [sem(f"x1_stored{k}") for k in range(2)]
        typed_ready = sem("typed_ready")
        typedT_ps = sem("typedT_ps")
        typedT_ready = sem("typedT_ready")
        k_ps = sem("k_ps")
        q_ps = sem("q_ps")
        v_ps = sem("v_ps")
        kT_ready = sem("kT_ready")
        kw_ps = sem("kw_ps")
        kw_low = sem("kw_low")
        kw_high = sem("kw_high")
        row_stored = [sem(f"row_stored{k}") for k in range(2)]
        l1_start = sem("l1_start")
        l1_tables = sem("l1_tables")
        l1_idx = sem("l1_idx")
        l1_rows = [sem(f"l1_rows{u}") for u in range(SLOTS1)]
        l1_free = [sem(f"l1_free{u}") for u in range(SLOTS1)]
        away_ready = sem("away_ready")
        away_used = sem("away_used")
        queries_ready = sem("queries_ready")
        keysT_ps = sem("keysT_ps")
        keysT_ready = sem("keysT_ready")
        score_ps = sem("score_ps")
        max_ready = sem("max_ready")
        prob_ready = sem("prob_ready")
        probT_ps = sem("probT_ps")
        prob_copied = sem("prob_copied")
        spread_ready = sem("spread_ready")
        rep_ps = sem("rep_ps")
        part_ps = sem("part_ps")
        delta_ready = sem("delta_ready")
        factor_ready = sem("factor_ready")
        l1_vec = sem("l1_vec")
        l1_done = sem("l1_done")
        c_start = sem("c_start")
        attn_ready = sem("attn_ready")
        attn_ps = sem("attn_ps")
        c_var = sem("c_var")
        c_std = sem("c_std")
        c_shift = sem("c_shift")
        c_vec = sem("c_vec")
        y_ready = sem("y_ready")
        stored = sem("stored")

        block = ctx.enter_context(nc.Block())

        def gate(e, s, value):
            e.wait_ge(s, value)
            e.sem_inc(gates_passed, 1)

        def passes(e):
            e.wait_ge(passes_ready, 1)
            return e.value_load(passes_i[0:1, 0:1], min_val=1, max_val=NPASS)

        PAIRS = [-(-(TILES - v) // 2) for v in range(2)]
        TURNS = [-(-(NBLK - u) // SLOTS1) for u in range(SLOTS1)]

        def first_sweep(e, ps_, body):
            def pair_(i, v, half):
                return Pair(ps_ * NBLK + i * 2, i * 2, v, ps_ * PAIRS[v] + half)

            def tile(t, k, half):
                return Tile(ps_ * TILES + t, t, k, ps_ * PAIRS[k] + half)

            body(pair_(0, 0, 0), None)
            body(pair_(1, 1, 0), None)
            with e.Fori(0, (TILES - 3) // 2) as q:
                for v in range(2):
                    body(pair_(q * 2 + 2 + v, v, q + 1), tile(q * 2 + v, v, q))
            body(pair_(TILES - 1, 0, TILES // 2), tile(TILES - 3, 0, TILES // 2 - 1))
            body(None, tile(TILES - 2, 1, TILES // 2 - 1))
            body(None, tile(TILES - 1, 0, TILES // 2))

        def second_sweep(e, ps_, body):
            def blk(b, u, turn):
                return Block(ps_ * NBLK + b, b, u, ps_ * TURNS[u] + turn)

            body(blk(0, 0, 0), None)
            with e.Fori(0, NBLK // SLOTS1) as i:
                for v in range(SLOTS1):
                    u = (v + 1) % SLOTS1
                    body(blk(i * SLOTS1 + v + 1, u, i + (v + 1) // SLOTS1), blk(i * SLOTS1 + v, v, i))
            body(blk(NBLK - 1, 1, NBLK // SLOTS1), blk(NBLK - 2, 0, NBLK // SLOTS1))
            body(None, blk(NBLK - 1, 1, NBLK // SLOTS1))

        def chunks(e, body):
            with e.Fori(0, CHUNKS // 2) as q:
                for k in range(2):
                    body(q * 2 + k, k)
            body(CHUNKS - 1, 0)

        def load_edges(e, tile, dram, s):
            e.dma_start(tile[:, 0:FULL * RUN].rearrange("p (h j) -> p h j", j=RUN),
                        dram[0:FULL * HALF].rearrange("(h p j) -> p h j", p=P, j=RUN)).then_inc(s, 16)
            e.dma_start(tile[0:REST // RUN, FULL * RUN:EDGE_COLS],
                        dram[FULL * HALF:E].rearrange("(p j) -> p j", j=RUN)).then_inc(s, 16)

        @block.sync
        def _(sp):
            sp.wait_ge(pads_ready, 3)
            load_edges(sp, dst_i, dst, L["dst"])
            load_edges(sp, src_idx[:, 0:EDGE_COLS].bitcast(I32), src, L["src"])
            load_edges(sp, etype_i, etype, L["etype"])
            sp.dma_start(w0_s, w0[:, :]).then_inc(L["weights"], 16)
            for w_s, w in ((wq_s, wq), (wk_s, wk), (wv_s, wv), (we_s, we)):
                sp.dma_start(w_s, w.rearrange("t i o -> i t o")).then_inc(L["weights"], 16)
            for k in range(2):
                sp.sem_inc(row_stored[k], 16)
                sp.sem_inc(x1_stored[k], 16)
            count = passes(sp)

            def load_x(t, k, rows=P):
                sp.dma_start(x_tile[k][0:rows, :], x[bass.ds(t * P, rows), :]).then_inc(x_loaded[k], 16)

            def store(tile):
                gate(sp, x1_ready, tile.n + 1)
                sp.dma_start(x1_dram[bass.ds(tile.t * P, P), :], x1_tile[tile.k]).then_inc(x1_stored[tile.k], 16)
                gate(sp, kw_low, tile.n + 1)
                gate(sp, kw_high, tile.n + 1)
                sp.dma_start(table_rows[bass.ds(tile.t * P, P), :], kv_rows[tile.k].rearrange("p e c -> p (e c)")
                             ).then_inc(row_stored[tile.k], 16)

            with sp.Fori(0, count) as ps_:
                load_x(0, 0)
                with sp.Fori(0, (TILES - 3) // 2) as q:
                    for k in range(2):
                        load_x(q * 2 + k + 1, 1 - k)
                        store(Tile(ps_ * TILES + q * 2 + k, q * 2 + k, k, None))
                for t in range(TILES - 3, TILES):
                    if t + 1 < TILES:
                        load_x(t + 1, (t + 1) % 2, P if t + 2 < TILES else LAST)
                    store(Tile(ps_ * TILES + t, t, t % 2, None))

            for k in range(2):
                sp.wait_ge(row_stored[k], count * (16 * PAIRS[k]) + 16)
                sp.wait_ge(x1_stored[k], count * (16 * PAIRS[k]) + 16)
            sp.sem_inc(l1_start, 1)
            sp.wait_ge(l1_done, 1)
            sp.dma_start(x1_nodes, x1_view).then_inc(L["x1"], 16)
            o_full = out[0:(TILES - 1) * P, :].rearrange("(t p) d -> p t d", p=P)
            with sp.Fori(0, CHUNKS - 1) as c:
                sp.wait_ge(y_ready, c + 1)
                sp.dma_start(o_full[:, bass.ds(c * CH, CH), :], x1_nodes[:, bass.ds(c * CH, CH), :]).then_inc(stored, 16)
            sp.wait_ge(y_ready, CHUNKS)
            sp.dma_start(o_full[:, TILES - CH:TILES - 1, :], x1_nodes[:, TILES - CH:TILES - 1, :]).then_inc(stored, 16)
            sp.dma_start(out[(TILES - 1) * P:N, :], x1_nodes[0:LAST, TILES - 1, :]).then_inc(stored, 16)
            sp.wait_ge(stored, 16 * (CHUNKS + 1))

        @block.gpsimd
        def _(pool):
            tail = slice(FULL * RUN, EDGE_COLS)
            pool.memset(dst_i[:, tail], -4096).then_inc(pads_ready, 1)
            pool.memset(src_idx[:, FULL * RUN:], 0).then_inc(pads_ready, 1)
            pool.memset(etype_i[:, tail], 0).then_inc(pads_ready, 1)
            pool.iota(iota_i[:, :], pattern=[[1, WIN]], base=0, channel_multiplier=0).then_inc(consts_ready, 1)
            pool.iota(bound_i[:, :], pattern=[[P, NHALF // 4], [0, 4]], base=-P, channel_multiplier=0
                      ).then_inc(consts_ready, 1)
            pool.memset(identf[:, :], 0.0).then_inc(pool_step, 1)
            pool.wait_ge(pool_step, 1)
            pool.affine_select(out=identf[:, :], in_=identf[:, :], compare_op=ALU.not_equal, fill=1.0, base=0,
                               pattern=[[-1, P]], channel_multiplier=1).then_inc(consts_ready, 1)
            pool.memset(onesf[:, :], 1.0).then_inc(consts_ready, 1)
            pool.memset(onesb[:, :], 1.0).then_inc(consts_ready, 1)
            pool.memset(eps_col[:, :], LN_EPS).then_inc(consts_ready, 1)
            pool.memset(key_idx[:, EDGE_COLS:], 0).then_inc(consts_ready, 1)
            pool.memset(queries_all[:, NPAD:NACC], 0.0).then_inc(consts_ready, 1)
            pool.dma_start(ntype_i[:, 0:TILES - 1], ntype[0:(TILES - 1) * P].rearrange("(t p) -> p t", p=P),
                           allow_slow_non_contiguous=True).then_inc(L["small"], 16)
            pool.dma_start(ntype_i[0:LAST, TILES - 1:TILES], ntype[(TILES - 1) * P:N].rearrange("(p t) -> p t", t=1)
                           ).then_inc(L["small"], 16)
            pool.dma_start(bias_c[:, :], b0.rearrange("(d a) -> d a", a=1)).then_inc(L["small"], 16)
            pool.dma_start(mu_b[:, :], mu.rearrange("(a d) -> a d", a=1).broadcast_to([P, ET])).then_inc(L["small"], 16)
            count = passes(pool)

            def gather(rows, table_, j, u, s):
                pool.indirect_dma_start(rows[u][:, j, :], None, table_,
                                        bass.IndirectOffsetOnAxis(ap=stage[:, u, j:j + 1], axis=0)).then_inc(s[u], 16)

            def l0(ps_, i, u):
                gate(pool, l0_idx, ps_ * (TILES + 1) + i * 2 + u // 2 + 1)
                gate(pool, l0_free[u], ps_ * PAIRS[u // 2] + i + 1)
                for j in range(COLS):
                    gather(x_ring, x, j, u, l0_rows)

            def l1(ps_, i, u):
                gate(pool, l1_idx, ps_ * (NBLK + 2) + i * SLOTS1 + u + 1)
                gate(pool, l1_free[u], ps_ * TURNS[u] + i + 1)
                for j in range(COLS):
                    gather(kv_ring, table, j, u, l1_rows)

            for slots, body in ((SLOTS0, l0), (SLOTS1, l1)):
                with pool.Fori(0, count) as ps_:
                    with pool.Fori(0, NBLK // slots) as i:
                        for u in range(slots):
                            body(ps_, i, u)
                    for u in range(NBLK % slots):
                        body(ps_, NBLK // slots, u)
                if body is l0:
                    pool.wait_ge(l1_start, 1)

        @block.tensor
        def _(pe):
            pe.wait_ge(consts_ready, 8)
            pe.wait_ge(dst_ready, 1)
            pe.matmul(bank[0][:, 0:NHALF], onesf[0:1, :],
                      dst_f[0:1, :].rearrange("p (h j) -> p h j", j=RUN)[:, :, 0], start=True, stop=True
                      ).then_inc(first_ps, 1)
            pe.wait_ge(inside_ready, 1)
            pe.matmul(bank[1][:, 0:1], onesf[:, :], plan[:, 0:1], start=True, stop=True).then_inc(inside_ps, 1)
            pe.wait_ge(L["weights"], 80)
            pe.transpose(bank[2][:, 0:P], w0_s[:, 0:D], identf[:, :])
            pe.transpose(bank[2][:, P:2 * P], w0_s[:, D:2 * D], identf[:, :]).then_inc(w0_ps, 1)
            pe.wait_ge(w0_ready, 1)
            count = passes(pe)

            def sum_block(pair_, o):
                u = 2 * pair_.v + o
                pe.wait_ge(hot_ready, pair_.it + o + 1)
                pe.wait_ge(l0_rows[u], (pair_.turn + 1) * (16 * COLS))
                for h in range(2):
                    for what in range(2):
                        at = (h * 2 + what) * WIN
                        for j in range(RUN):
                            mm = pe.matmul(bank[o][:, at:at + WIN],
                                           onesb[:, :] if what else x_ring[u][:, h * RUN + j, :],
                                           (hot_b if what else hot)[o][:, h * RUN + j, :],
                                           start=(j == 0), stop=(j == RUN - 1))
                mm.then_inc(l0_part, 1)

            def transpose_x(tile):
                pe.wait_ge(x_loaded[tile.k], (tile.turn + 1) * 16)
                pe.transpose(bank[2][:, 0:P], x_tile[tile.k], identf[:, :]).then_inc(xT_ps, 1)

            def first_product(tile):
                pe.wait_ge(xT_copied, tile.n + 1)
                pe.wait_ge(mean_ready, tile.n + 1)
                pe.matmul(bank[2][:, 0:P], w0T[:, 0, :], xT, start=True, stop=False)
                pe.matmul(bank[2][:, 0:P], w0T[:, 1, :], meanT, start=False, stop=True).then_inc(reluT_ps, 1)
                pe.wait_ge(relu_ready, tile.n + 1)
                pe.transpose(bank[2][:, 0:P], reluT, identf[:, :]).then_inc(relu_ps, 1)

            def project(tile):
                pe.wait_ge(typed_ready, tile.n + 1)
                for t in range(NT):
                    tr = pe.transpose(bank[3][:, t * P:(t + 1) * P], x1_typed[:, t, :], identf[:, :])
                tr.then_inc(typedT_ps, 1)
                pe.wait_ge(typedT_ready, tile.n + 1)
                for t in range(NT):
                    mm = pe.matmul(bank[4][:, 0:P], wk_s[:, t, :], x1_typedT[:, t, :], start=(t == 0), stop=(t == NT - 1))
                mm.then_inc(k_ps, 1)
                for t in range(NT):
                    mm = pe.matmul(bank[5][:, 0:P], wq_s[:, t, :], x1_typedT[:, t, :], start=(t == 0), stop=(t == NT - 1))
                mm.then_inc(q_ps, 1)
                for t in range(NT):
                    mm = pe.matmul(bank[6][:, 0:P], x1_typedT[:, t, :], wv_s[:, t, :], start=(t == 0), stop=(t == NT - 1))
                mm.then_inc(v_ps, 1)
                pe.wait_ge(kT_ready, tile.n + 1)
                pe.matmul(bank[7], kT, we_s[:, 0:4, :], start=True, stop=True)
                pe.matmul(bank[3], kT, we_s[:, 4:8, :], start=True, stop=True).then_inc(kw_ps, 1)

            def l0(pair_, tile):
                if tile:
                    transpose_x(tile)
                if pair_:
                    sum_block(pair_, 0)
                if tile:
                    first_product(tile)
                if pair_:
                    sum_block(pair_, 1)
                if tile:
                    project(tile)

            with pe.Fori(0, count) as ps_:
                first_sweep(pe, ps_, l0)

            scores, probs = pair[1], pair[2]

            def mask(new):
                pe.wait_ge(away_ready, new.it + 1)
                for h in range(2):
                    for q in range(2):
                        for j in range(4):
                            at = q * 512 + j * P
                            mm = pe.matmul(scores[h * WIN:(h + 1) * WIN, at:at + P], away[:, h * RUN + q * 4 + j, :],
                                      negid[:, :], start=(j == 0), stop=False, skip_group_check=True)
                mm.then_inc(away_used, 1)

            def score(old):
                pe.wait_ge(queries_ready, old.it + 1)
                for g in range(4):
                    h, q = g // 2, g % 2
                    pe.wait_ge(keysT_ready, old.it * 4 + g + 1)
                    mm = pe.matmul(scores[h * WIN:(h + 1) * WIN, q * 512:(q + 1) * 512], queries[:, h, :],
                                   keysT[:, g, :], start=False, stop=True, skip_group_check=True)
                mm.then_inc(score_ps, 1)

            def transpose_keys(new):
                pe.wait_ge(l1_rows[new.u], (new.turn + 1) * (16 * COLS))
                for g in range(4):
                    if g >= 2:
                        pe.wait_ge(keysT_ready, new.it * 4 + g - 1)
                    for j in range(4):
                        tr = pe.transpose(bank[g % 2][:, j * P:(j + 1) * P], kv_ring[new.u][:, g * 4 + j, 0:D],
                                          identf[:, :])
                    tr.then_inc(keysT_ps, 1)

            def l1(new, old):
                if old:
                    score(old)
                if new:
                    transpose_keys(new)
                if old:
                    pe.wait_ge(prob_ready, old.it + 1)
                    for j in range(RUN):
                        tr = pe.transpose(probs[:, j * P:(j + 1) * P], probT[:, j * P:(j + 1) * P], identf[:, :])
                    tr.then_inc(probT_ps, 1)
                    pe.wait_ge(spread_ready, old.it + 1)
                    pe.matmul(bank[7][:, 0:P], onesf[:, :], spread[:, 0, :], start=True, stop=True).then_inc(rep_ps, 1)
                    for h in range(2):
                        pe.matmul(bank[6][:, (2 * h + 1) * WIN:(2 * h + 2) * WIN], onesf[:, :],
                                  spread[:, 1, h * WIN:(h + 1) * WIN], start=True, stop=True)
                if new:
                    mask(new)
                if old:
                    pe.wait_ge(prob_copied, old.it + 1)
                    for h in range(2):
                        for j in range(RUN):
                            mm = pe.matmul(bank[6][:, 2 * h * WIN:(2 * h + 1) * WIN], kv_ring[old.u][:, h * RUN + j, D:2 * D],
                                           prob[:, j, h * WIN:(h + 1) * WIN], start=(j == 0), stop=(j == RUN - 1))
                    mm.then_inc(part_ps, 1)

            with pe.Fori(0, count) as ps_:
                second_sweep(pe, ps_, l1)
            pe.drain().then_inc(l1_done, 1)

            def rows_back(c, k):
                pe.wait_ge(attn_ready, c + 1)
                for t in range(CH):
                    pe.transpose(pair[0][:, t * P:(t + 1) * P], attn[:, t * P:(t + 1) * P], identf[:, :])
                for t in range(CH):
                    mm = pe.matmul(bank[2][:, t:t + 1], attn_sum[0:1, t * P:(t + 1) * P], onesf[0:1, 0:1],
                                   start=True, stop=True)
                mm.then_inc(attn_ps, 1)

            chunks(pe, rows_back)

        @block.scalar
        def _(act):
            act.wait_ge(w0_ps, 1)
            act.activation(w0T[:, :, :], by_type(bank[2][:, 0:2 * P]), ACT.Copy).then_inc(w0_ready, 1)
            act.wait_ge(L["small"], 64)
            act.wait_ge(L["src"], 32)
            count = passes(act)

            def tile_start(tile):
                act.wait_ge(xT_ps, tile.n + 1)
                act.activation(xT, bank[2][:, 0:P], ACT.Copy).then_inc(xT_copied, 1)
                act.wait_ge(reluT_ps, tile.n + 1)
                act.activation(reluT, bank[2][:, 0:P], ACT.Relu, bias=bias_c[:, 0:1]).then_inc(relu_ready, 1)
                act.wait_ge(var_ready, tile.n + 1)
                act.activation(std[:, 0, 0:1], aggr[:, 0, 0, 1:2], ACT.Sqrt, bias=eps_col[:, 0:1]).then_inc(std_ready, 1)

            def project(tile):
                act.wait_ge(typedT_ps, tile.n + 1)
                act.activation(x1_typedT, by_type(bank[3]), ACT.Copy).then_inc(typedT_ready, 1)
                act.wait_ge(k_ps, tile.n + 1)
                act.activation(kT, bank[4][:, 0:P], ACT.Copy).then_inc(kT_ready, 1)
                act.wait_ge(q_ps, tile.n + 1)
                act.activation(queries_all[:, bass.ds(tile.t * P, P)], bank[5][:, 0:P], ACT.Copy)
                act.wait_ge(row_stored[tile.k], (tile.turn + 1) * 16)
                act.wait_ge(v_ps, tile.n + 1)
                act.activation(kv_rows[tile.k][:, :, D:2 * D], bank[6][:, 0:P].unsqueeze(1).broadcast_to([P, ET, D]),
                               ACT.Copy)
                act.wait_ge(kw_ps, tile.n + 1)
                act.activation(kv_rows[tile.k][:, 4:8, 0:D], by_type(bank[3]), ACT.Copy).then_inc(kw_high, 1)

            def stage_pair(v, b):
                act.activation(stage[:, 2 * v:2 * v + 2, :].bitcast(I32).rearrange("p a b -> p (a b)"),
                               src_idx[:, bass.ds(b * COLS, 2 * COLS)].bitcast(I32), ACT.Copy).then_inc(l0_idx, 1)

            def l0(pair_, tile):
                if pair_:
                    if not isinstance(pair_.b, int) or pair_.b > 0:
                        gate(act, l0_part, pair_.it)
                    stage_pair(1 - pair_.v, pair_.b + 2)
                if tile:
                    tile_start(tile)
                    project(tile)

            with act.Fori(0, count) as ps_:
                stage_pair(0, 0)
                first_sweep(act, ps_, l0)
            act.wait_ge(keys_ready, 1)

            def stage_block(u, b):
                act.activation(stage[:, u, :].bitcast(I32), key_idx[:, bass.ds(b * COLS, COLS)].bitcast(I32), ACT.Copy
                               ).then_inc(l1_idx, 1)

            def copy_keys(new, gs):
                for g in gs:
                    act.wait_ge(keysT_ps, new.it * 4 + g + 1)
                    act.activation(keysT[:, g, :], bank[g % 2], ACT.Copy).then_inc(keysT_ready, 1)

            def l1(new, old):
                if new:
                    stage_block((new.u + 2) % SLOTS1, new.b + 2)
                    copy_keys(new, (0, 1))
                if old:
                    act.wait_ge(max_ready, old.it + 1)
                    act.activation(probT[:, :], pair[1], ACT.Exp, bias=cols[:, 1:2], accum_out=cols[:, 2:3]
                                   ).then_inc(prob_ready, 1)
                if new:
                    copy_keys(new, (2, 3))
                if old:
                    for h in range(2):
                        act.wait_ge(delta_ready, old.it * 2 + h + 1)
                        act.activation(factor[:, :, :], delta[:, :, :], ACT.Exp).then_inc(factor_ready, 1)

            with act.Fori(0, count) as ps_:
                stage_block(0, 0)
                stage_block(1, 1)
                second_sweep(act, ps_, l1)

            act.wait_ge(c_start, 1)

            def take(c):
                w = bass.ds(c * CW, CW)
                act.activation(attn_sum[0:1, :], sums[0:1, 1, w], ACT.Copy)
                act.activation(attn, sums[:, 0, w], ACT.Copy).then_inc(attn_ready, 1)

            def normalise(c, k):
                act.wait_ge(c_var, c + 1)
                act.activation(std[:, k, :], aggr[:, k, :, 1], ACT.Sqrt, bias=eps_col[:, 0:1]).then_inc(c_std, 1)
                if not isinstance(c, int):
                    take(c + 1)
                act.wait_ge(c_shift, c + 1)
                for t in range(CH):
                    ins = act.activation(queries_all[:, bass.ds(c * CW + t * P, P)], y_rows[k][:, t * P:(t + 1) * P],
                                         ACT.Identity, bias=shift[:, k, t:t + 1], scale=std[:, k, t:t + 1])
                ins.then_inc(y_ready, 1)

            take(0)
            chunks(act, normalise)

        @block.vector
        def _(dve):
            steps = [0]

            def setup(ins):
                steps[0] += 1
                ins.then_inc(setup_vec, 1)
                dve.wait_ge(setup_vec, steps[0])

            edges = lambda t: t.rearrange("p (h j) -> p h j", j=RUN)
            over = lambda t: t[:, :].unsqueeze(2).broadcast_to([P, NHALF, RUN])
            dve.wait_ge(L["dst"], 32)
            setup(dve.tensor_copy(dst_f[:, :], dst_i))
            dve.sem_inc(dst_ready, 1)
            dve.wait_ge(consts_ready, 8)
            dve.tensor_copy(iota_f[:, :], iota_i[:, :])
            dve.tensor_scalar(negid[:, :], identf[:, :], NEG, None, ALU.mult)
            dve.memset(plan[:, 3:4], 0.0)
            dve.wait_ge(first_ps, 1)
            setup(dve.tensor_copy(first[:, :], bank[0][:, 0:NHALF]))
            test, low = ring[:, 0:EDGE_COLS], base_f
            dve.tensor_tensor(low[:, :], first[:, :], bound_i[:, :], ALU.is_ge)
            setup(dve.tensor_tensor(edges(rel[:, :]), edges(dst_f[:, :]), over(first), ALU.subtract))
            setup(dve.tensor_scalar(test, rel[:, :], float(WIN), None, ALU.is_lt))
            setup(dve.scalar_tensor_tensor(test, rel[:, :], 0.0, test, ALU.is_ge, ALU.mult))
            setup(dve.tensor_tensor(edges(test), edges(test), over(low), ALU.mult))
            setup(dve.reduce_sum(plan[:, 0:1], test, AX))
            dve.sem_inc(inside_ready, 1)
            dve.wait_ge(inside_ps, 1)
            setup(dve.tensor_scalar(plan[:, 1:2], bank[1][:, 0:1], float(E), None, ALU.is_equal))
            dve.tensor_scalar(plan[:, 2:3], plan[:, 1:2], -float(WIN), float(WIN), ALU.mult, ALU.add)
            setup(dve.tensor_scalar(passes_i[0:1, 0:1], plan[0:1, 1:2], float(1 - NPASS), float(NPASS), ALU.mult, ALU.add))
            dve.sem_inc(passes_ready, 1)
            count = passes(dve)
            dve.memset(sums[:, :, :], 0.0)
            dve.wait_ge(L["etype"], 32)
            dve.wait_ge(L["src"], 32)
            dve.wait_ge(L["small"], 64)
            dve.wait_ge(L["weights"], 80)
            dve.scalar_tensor_tensor(key_idx[:, 0:EDGE_COLS], src_idx[:, 0:EDGE_COLS].bitcast(I32), float(ET), etype_i,
                                     ALU.mult, ALU.add)
            setup(dve.memset(ntype_m[:, TILES - 1, :], 0.0))
            for t in range(NT):
                dve.tensor_scalar(ntype_m[:, 0:TILES - 1, t], ntype_i[:, 0:TILES - 1], float(t), None, ALU.is_equal)
                dve.tensor_scalar(ntype_m[0:LAST, TILES - 1, t:t + 1], ntype_i[0:LAST, TILES - 1:TILES], float(t), None,
                                  ALU.is_equal)
            for e in range(ET):
                ins = dve.tensor_scalar(we_s[:, e, :], we_s[:, e, :], mu_b[:, e:e + 1], SCALE, ALU.mult, ALU.mult)
            setup(ins)
            dve.sem_inc(keys_ready, 1)
            dve.sem_inc(l0_added, 1)
            for u in range(SLOTS0):
                dve.sem_inc(l0_free[u], 1)

            def tables(chain, ps_):
                dve.scalar_tensor_tensor(base_f[:, :], first[:, :], plan[:, 1:2],
                                         plan[:, 3:4].broadcast_to([P, NHALF]), ALU.mult, ALU.add).then_inc(chain, 1)
                dve.wait_ge(chain, ps_ * 3 + 1)
                dve.tensor_scalar(plan[:, 3:4], plan[:, 3:4], plan[:, 2:3], None, ALU.add).then_inc(chain, 1)
                dve.tensor_copy(base_i[0:1, :], base_f[0:1, :])
                dve.tensor_tensor(edges(rel[:, :]), edges(dst_f[:, :]), over(base_f), ALU.subtract).then_inc(chain, 1)
                gate(dve, chain, ps_ * 3 + 3)

            def member(out_, b, op):
                return dve.tensor_tensor(
                    out_, rel[:, bass.ds(b * COLS, COLS)].unsqueeze(2).broadcast_to([P, COLS, WIN]),
                    iota_f[:, :].unsqueeze(1).broadcast_to([P, COLS, WIN]), op)

            def bases(b):
                return [dve.value_load(base_i[0:1, bass.ds(b * 2 + h, 1)], min_val=0, max_val=NPAD) for h in range(2)]

            def find_nodes(pair_, o):
                member(hot_b[o], pair_.b + o, ALU.is_equal)
                member(hot[o], pair_.b + o, ALU.is_equal).then_inc(hot_ready, 1)

            def add_block(pair_, o):
                base = bases(pair_.b + o)
                dve.wait_ge(l0_part, pair_.it + o + 1)
                dve.sem_inc(l0_free[2 * pair_.v + o], 1)
                for h in range(2):
                    dve.wait_ge(l0_added, (pair_.it + o) * 2 + h + 1)
                    win = sums[:, :, bass.ds(base[h], WIN)]
                    dve.tensor_tensor(win, bank[o][:, h * 2 * WIN:(h + 1) * 2 * WIN].rearrange("p (a w) -> p a w", w=WIN),
                                      win, ALU.add).then_inc(l0_added, 1)

            def mean(tile, added):
                w = bass.ds(tile.t * P, P)

                def link(ins, k):
                    ins.then_inc(tile_vec, 1)
                    dve.wait_ge(tile_vec, tile.n * 6 + k)
                dve.wait_ge(l0_added, added)
                link(dve.tensor_scalar(inverse, sums[:, 1, w], 1.0, None, ALU.max), 1)
                link(dve.reciprocal(inverse, inverse), 2)
                dve.tensor_tensor(summed, sums[:, 0, w], inverse, ALU.mult)
                dve.wait_ge(xT_copied, tile.n + 1)
                link(dve.scalar_tensor_tensor(alone, sums[:, 1, w], 0.0, xT, ALU.is_equal, ALU.mult), 3)
                dve.tensor_tensor(meanT, summed, alone, ALU.add).then_inc(mean_ready, 1)

            def norm_x1(tile):
                def link(ins, k):
                    ins.then_inc(tile_vec, 1)
                    dve.wait_ge(tile_vec, tile.n * 6 + k)
                dve.wait_ge(relu_ps, tile.n + 1)
                link(dve.tensor_tensor(summed, bank[2][:, 0:P], x_tile[tile.k], ALU.add), 4)
                dve.bn_stats(stats[:, 0, :], summed).then_inc(tile_vec, 1)
                gate(dve, tile_vec, tile.n * 6 + 5)
                dve.bn_aggr(aggr[:, 0, 0, :], stats[:, 0, :]).then_inc(var_ready, 1)
                dve.wait_ge(std_ready, tile.n + 1)
                link(dve.reciprocal(std[:, 0, 0:1], std[:, 0, 0:1]), 6)
                dve.wait_ge(x1_stored[tile.k], (tile.turn + 1) * 16)
                dve.tensor_scalar(x1_tile[tile.k], summed, aggr[:, 0, 0, 0:1], std[:, 0, 0:1], ALU.subtract, ALU.mult
                                  ).then_inc(x1_ready, 1)
                dve.wait_ge(x1_ready, tile.n + 1)
                for t in range(NT):
                    m = ntype_m[:, bass.ds(tile.t, 1), t:t + 1].rearrange("p a b -> p (a b)")
                    ins = dve.tensor_scalar(x1_typed[:, t, :], x1_tile[tile.k], m, None, ALU.mult)
                ins.then_inc(typed_ready, 1)

            def copy_rows(tile):
                dve.wait_ge(kw_ps, tile.n + 1)
                dve.wait_ge(row_stored[tile.k], (tile.turn + 1) * 16)
                dve.tensor_copy(kv_rows[tile.k][:, 0:4, 0:D], by_type(bank[7])).then_inc(kw_low, 1)

            with dve.Fori(0, count) as ps_:
                tables(l0_tables, ps_)

                def l0(pair_, tile):
                    if pair_:
                        find_nodes(pair_, 0)
                    if tile:
                        mean(tile, pair_.it * 2 + 1 if pair_ else (ps_ + 1) * (2 * NBLK) + 1)
                    if pair_:
                        find_nodes(pair_, 1)
                        add_block(pair_, 0)
                    if tile:
                        norm_x1(tile)
                    if pair_:
                        add_block(pair_, 1)
                    if tile:
                        copy_rows(tile)

                first_sweep(dve, ps_, l0)

            dve.memset(sums[:, :, :], 0.0)
            setup(dve.memset(plan[:, 3:4], 0.0))
            for u in range(SLOTS1):
                dve.sem_inc(l1_free[u], 1)
            dve.sem_inc(away_used, 1)

            def l1(new, old):
                if new:
                    new_base = bases(new.b)
                if old:
                    base = bases(old.b)
                K = 9
                k = [0]

                def link(ins):
                    k[0] += 1
                    ins.then_inc(l1_vec, 1)
                    dve.wait_ge(l1_vec, old.it * K + k[0])

                def take_queries():
                    for h in range(2):
                        ins = dve.tensor_copy(queries[:, h, :], queries_all[:, bass.ds(new_base[h], WIN)])
                    ins.then_inc(queries_ready, 1)

                if new:
                    dve.wait_ge(away_used, new.it + 1)
                    member(away[:, :, :], new.b, ALU.not_equal).then_inc(away_ready, 1)
                if not old:
                    take_queries()
                    return
                dve.wait_ge(score_ps, old.it + 1)
                link(dve.reduce_max(cols[:, 0:1], pair[1], AX))
                dve.tensor_scalar(cols[:, 1:2], cols[:, 0:1], FLOOR, -1.0, ALU.max, ALU.mult).then_inc(max_ready, 1)
                if new:
                    take_queries()
                dve.wait_ge(max_ready, old.it + 1)
                dve.tensor_scalar(spread[:, 0, :], identf[:, :], cols[:, 1:2], None, ALU.mult)
                dve.wait_ge(prob_ready, old.it + 1)
                dve.tensor_scalar(spread[:, 1, :], identf[:, :], cols[:, 2:3], None, ALU.mult).then_inc(spread_ready, 1)
                dve.wait_ge(probT_ps, old.it + 1)
                dve.tensor_copy(prob[:, :, :].rearrange("p a b -> p (a b)"), pair[2]).then_inc(prob_copied, 1)
                dve.wait_ge(rep_ps, old.it + 1)
                for h in range(2):
                    win = bass.ds(base[h], WIN)
                    new_max = bank[7][:, h * WIN:(h + 1) * WIN]
                    link(dve.tensor_tensor(larger[:, :], new_max, negmax[:, win], ALU.min))
                    dve.tensor_tensor(delta[:, 0, :], larger[:, :], negmax[:, win], ALU.subtract)
                    dve.tensor_tensor(delta[:, 1, :], larger[:, :], new_max, ALU.subtract).then_inc(delta_ready, 1)
                    gate(dve, delta_ready, old.it * 2 + h + 1)
                    link(dve.tensor_copy(negmax[:, win], larger[:, :]))
                    dve.wait_ge(factor_ready, old.it * 2 + h + 1)
                    dve.tensor_tensor(scaled[:, 0, :, :], sums[:, :, win],
                                      factor[:, 0, :].unsqueeze(1).broadcast_to([P, 2, WIN]), ALU.mult)
                    if h == 0:
                        dve.wait_ge(part_ps, old.it + 1)
                        dve.sem_inc(l1_free[old.u], 1)
                    link(dve.tensor_tensor(scaled[:, 1, :, :],
                                           bank[6][:, h * 2 * WIN:(h + 1) * 2 * WIN].rearrange("p (a w) -> p a w", w=WIN),
                                           factor[:, 1, :].unsqueeze(1).broadcast_to([P, 2, WIN]), ALU.mult))
                    link(dve.tensor_tensor(sums[:, :, win], scaled[:, 0, :, :], scaled[:, 1, :, :], ALU.add))
                assert k[0] == K
                dve.sem_inc(gates_passed, 1)

            dve.wait_ge(l1_start, 1)
            setup(dve.memset(negmax[:, :], -FLOOR))
            with dve.Fori(0, count) as ps_:
                tables(l1_tables, ps_)
                second_sweep(dve, ps_, l1)
            dve.sem_inc(c_start, 1)

            dve.wait_ge(L["x1"], 16)

            def last(c, k):
                def link(ins, j):
                    ins.then_inc(c_vec, 1)
                    dve.wait_ge(c_vec, c * 5 + j)
                dve.wait_ge(attn_ps, c + 1)
                link(dve.tensor_scalar(weight[:, :], bank[2][:, 0:CH], SUM_EPS, None, ALU.add), 1)
                link(dve.reciprocal(weight[:, :], weight[:, :]), 2)
                for t in range(CH):
                    ins = dve.scalar_tensor_tensor(y_rows[k][:, t * P:(t + 1) * P], pair[0][:, t * P:(t + 1) * P],
                                                   weight[:, t:t + 1], queries_all[:, bass.ds(c * CW + t * P, P)],
                                                   ALU.mult, ALU.add)
                link(ins, 3)
                for t in range(CH):
                    ins = dve.bn_stats(stats[:, t, :], y_rows[k][:, t * P:(t + 1) * P])
                ins.then_inc(c_vec, 1)
                gate(dve, c_vec, c * 5 + 4)
                for t in range(CH):
                    ins = dve.bn_aggr(aggr[:, k, t, :], stats[:, t, :])
                ins.then_inc(c_var, 1)
                dve.wait_ge(c_std, c + 1)
                link(dve.reciprocal(std[:, k, :], std[:, k, :]), 5)
                dve.scalar_tensor_tensor(shift[:, k, :], aggr[:, k, :, 0], -1.0, std[:, k, :], ALU.mult, ALU.mult
                                         ).then_inc(c_shift, 1)

            chunks(dve, last)


_INS = ["x", "src", "dst", "edge_type_8", "node_type_4", "L0_gnn_W", "L0_gnn_b", "L1_gnn_W_Q", "L1_gnn_W_K",
        "L1_gnn_W_V", "L1_gnn_W_edge", "L1_gnn_mu"]


def kernel(**inputs):
    import numpy as _np
    import concourse.bacc as _bacc
    from concourse import mybir as _mybir
    from concourse.bass_utils import run_bass_kernel_spmd as _run

    nc = _bacc.Bacc("TRN2", target_bir_lowering=False, num_devices=1)
    arrays, args = {}, []
    for name in _INS:
        a = _np.ascontiguousarray(inputs[name])
        arrays[f"in_{name}_dram"] = a
        args.append(nc.dram_tensor(f"in_{name}_dram", a.shape, _mybir.dt.from_np(a.dtype), kind="ExternalInput").ap())
    args.append(nc.dram_tensor("out_0_dram", inputs["x"].shape, _mybir.dt.float32, kind="ExternalOutput").ap())
    gnn_kernel(nc, *args)
    r = _run(nc, [arrays], core_ids=[0])
    return r.results[0]["out_0_dram"]
```

```python
from collections import namedtuple
from contextlib import ExitStack

import concourse.bass as bass
from concourse import mybir

ALU = mybir.AluOpType
ACT = mybir.ActivationFunctionType
AX = mybir.AxisListType.X
F32 = mybir.dt.float32
BF16 = mybir.dt.bfloat16
I32 = mybir.dt.int32
U32 = mybir.dt.uint32

P = 128
RUN = 8
HALF = P * RUN
BLOCK = 2 * HALF
COLS = 2 * RUN
WIN = 64
SLOTS0 = 4
SLOTS1 = 3
NEG = -1.0e30
FLOOR = -1.0e9
LN_EPS = 1e-5
SUM_EPS = 1e-10

Pair = namedtuple("Pair", "it b v turn here")
Block = namedtuple("Block", "it b u turn here")
Tile = namedtuple("Tile", "n t k turn")
Group = namedtuple("Group", "n g k turn")


def gnn_kernel(nc, x, src, dst, etype, ntype, w0, b0, wq, wk, wv, we, mu, out):
    N, D = x.shape
    E = src.shape[0]
    NT = wq.shape[0]
    ET = we.shape[0]
    assert D == P and NT * D == 512 and ET * D == 1024
    TILES = -(-N // P)
    LAST = N - (TILES - 1) * P
    NPAD = TILES * P
    GROUPS = NPAD // WIN
    LAST_GROUP = N - (GROUPS - 1) * WIN
    NBLK = -(-E // BLOCK)
    NHALF = 2 * NBLK
    EDGE_COLS = NHALF * RUN
    FULL = E // HALF
    REST = E - FULL * HALF
    assert FULL == NHALF - 1 and REST % RUN == 0 and REST > 0
    assert NBLK == GROUPS and LAST_GROUP > 0 and NBLK % 4 == 2 and NBLK % SLOTS1 == 2
    NPASS = NPAD // WIN + 1
    NACC = NPAD + WIN
    SCALE = float(D) ** -0.5

    with ExitStack() as ctx:
        def sb(name, shape, dt=F32):
            return ctx.enter_context(nc.sbuf_tensor(name, shape, dt))

        def sem(name):
            return ctx.enter_context(nc.semaphore(name))

        table = nc.dram_tensor("kv_table", (NPAD * ET, 2 * D), F32, kind="Internal").ap()
        table_rows = table.rearrange("(n e) c -> n (e c)", e=ET)
        x1_dram = nc.dram_tensor("x1_rows", (NPAD, D), F32, kind="Internal").ap()

        sums = sb("sums", [P, 2, NACC])
        negmax = sb("negmax", [P, NACC])
        queries_all = sb("queries_all", [P, NACC])
        src_idx = sb("src_idx", [P, EDGE_COLS + 2 * COLS], U32)
        key_idx = sb("key_idx", [P, EDGE_COLS + 2 * COLS], U32)
        dst_f = sb("dst_f", [P, EDGE_COLS])
        rel = sb("rel", [P, EDGE_COLS])
        ring = sb("ring", [P, SLOTS1 * COLS * 2 * D])
        stage = sb("stage", [P, 4, COLS], U32)
        keysT = sb("keysT", [P, 4, 512])
        probT = sb("probT", [P, HALF])
        prob = sb("prob", [P, RUN, P])
        away = sb("away", [P, COLS, WIN], BF16)
        identf = sb("identf", [P, P])
        negid = sb("negid", [P, P], BF16)
        onesf = sb("onesf", [P, P])
        onesb = sb("onesb", [P, P], BF16)
        queries = sb("queries", [P, 2, WIN])
        iota_i = sb("iota_i", [P, WIN], I32)
        iota_f = sb("iota_f", [P, WIN])
        bound_i = sb("bound_i", [P, NHALF], I32)
        first = sb("first", [P, NHALF])
        base_f = sb("base_f", [P, NHALF])
        base_i = sb("base_i", [1, NHALF], I32)
        plan = sb("plan", [P, 4])
        passes_i = sb("passes_i", [1, 2], I32)
        cols = sb("cols", [P, 4])
        spread = sb("spread", [P, 2, P])
        larger = sb("larger", [P, WIN])
        delta = sb("delta", [P, 2, 2, WIN])
        factor = sb("factor", [P, 2, 2, WIN])
        scaled = sb("scaled", [P, 2, 2, WIN])
        bias_c = sb("bias_c", [P, 1])
        mu_b = sb("mu_b", [P, ET])
        ntype_i = sb("ntype_i", [P, TILES], I32)
        ntype_m = sb("ntype_m", [P, TILES, NT])
        stats = sb("stats", [P, 6])
        aggr = sb("aggr", [P, 2])
        rstd = sb("rstd", [P, 1])
        eps_col = sb("eps_col", [P, 1])

        dst_i = rel[:, :].bitcast(I32)
        etype_i = keysT[:, :, :].rearrange("p a b -> p (a b)").bitcast(I32)[:, 0:EDGE_COLS]
        flat_keysT = keysT[:, :, :].rearrange("p a b -> p (a b)")
        hot = [probT[:, :].rearrange("p (j w) -> p j w", w=WIN),
               prob[:, :, :].rearrange("p a b -> p (a b)").rearrange("p (j w) -> p j w", w=WIN)]
        hot_b = [away[:, :, :], flat_keysT.bitcast(BF16)[:, 0:COLS * WIN].rearrange("p (j w) -> p j w", w=WIN)]
        x_ring = [ring[:, u * COLS * D:(u + 1) * COLS * D].rearrange("p (j d) -> p j d", d=D) for u in range(SLOTS0)]
        kv_ring = [ring[:, u * COLS * 2 * D:(u + 1) * COLS * 2 * D].rearrange("p (j c) -> p j c", c=2 * D)
                   for u in range(SLOTS1)]

        def parts(tile, at, end):
            def part(n):
                at[0] += n
                assert at[0] <= end
                return tile[:, at[0] - n:at[0]]
            return part

        ring_part = parts(ring, [SLOTS0 * COLS * D], SLOTS1 * COLS * 2 * D)
        by_type = lambda t: t.rearrange("p (t d) -> p t d", d=D)
        wq_s, wk_s, wv_s = (by_type(ring_part(NT * D)) for _ in range(3))
        we_s = by_type(ring_part(ET * D))
        w0T = by_type(ring_part(2 * D))
        w0_s = ring_part(2 * D)
        x_tile = [ring_part(D) for _ in range(2)]
        x1_tile = [ring_part(D) for _ in range(2)]
        xT, meanT, reluT, kT = (ring_part(P) for _ in range(4))
        max_part = parts(negmax, [0], NACC)
        kv_rows = [max_part(ET * 2 * D).rearrange("p (e c) -> p e c", c=2 * D) for _ in range(2)]
        x1_typed = by_type(max_part(NT * D))
        x1_typedT = by_type(max_part(NT * D))
        inverse, alone, summed = (max_part(P) for _ in range(3))
        idx_part = parts(src_idx[:, :].bitcast(F32), [0], EDGE_COLS + 2 * COLS)
        attnT, attn_inverse = (idx_part(WIN) for _ in range(2))
        y_sum = idx_part(D)[0:WIN, :]
        x1_group = [idx_part(D)[0:WIN, :] for _ in range(SLOTS1)]
        y_group = [idx_part(D)[0:WIN, :] for _ in range(SLOTS1)]

        pairs = [ctx.enter_context(nc.psum_tensor(f"banks{i}", [P, 2, 512], F32)) for i in range(4)]
        bank = [pairs[i // 2][:, i % 2, :] for i in range(8)]
        pair = [b[:, :, :].rearrange("p a b -> p (a b)") for b in pairs]

        part = [bank[6][:, 0:2 * WIN], bank[7][:, P:P + 2 * WIN]]
        maxima = bank[7][:, 0:P]

        L = {n: sem("loaded_" + n) for n in ("src", "dst", "etype", "w0", "weights", "small")}
        x_loaded = [sem(f"x_loaded{k}") for k in range(2)]
        gates_passed = sem("gates_passed")
        consts_ready = sem("consts_ready")
        pool_step = sem("pool_step")
        pads_ready = sem("pads_ready")
        setup_vec = sem("setup_vec")
        dst_ready = sem("dst_ready")
        first_ps = sem("first_ps")
        inside_ready = sem("inside_ready")
        inside_ps = sem("inside_ps")
        passes_ready = sem("passes_ready")
        keys_ready = sem("keys_ready")
        w0_ps = sem("w0_ps")
        w0_ready = sem("w0_ready")
        l0_tables = sem("l0_tables")
        l0_idx = sem("l0_idx")
        l0_rows = [sem(f"l0_rows{u}") for u in range(2 * SLOTS0)]
        l0_free = [sem(f"l0_free{u}") for u in range(SLOTS0)]
        l0_taken = sem("l0_taken")
        l0_reset = sem("l0_reset")
        hot_ready = sem("hot_ready")
        l0_part = sem("l0_part")
        l0_added = sem("l0_added")
        tile_vec = sem("tile_vec")
        xT_ps = sem("xT_ps")
        xT_copied = sem("xT_copied")
        mean_ready = sem("mean_ready")
        reluT_ps = sem("reluT_ps")
        relu_ready = sem("relu_ready")
        relu_ps = sem("relu_ps")
        var_ready = sem("var_ready")
        std_ready = sem("std_ready")
        x1_ready = sem("x1_ready")
        x1_stored = [sem(f"x1_stored{k}") for k in range(2)]
        typed_ready = sem("typed_ready")
        typedT_ps = sem("typedT_ps")
        typedT_ready = sem("typedT_ready")
        k_ps = sem("k_ps")
        q_ps = sem("q_ps")
        q_copied = sem("q_copied")
        v_ps = sem("v_ps")
        kT_ready = sem("kT_ready")
        kw_ps = sem("kw_ps")
        kw_low = sem("kw_low")
        kw_high = sem("kw_high")
        row_stored = [sem(f"row_stored{k}") for k in range(2)]
        l1_start = sem("l1_start")
        l1_tables = sem("l1_tables")
        l1_idx = sem("l1_idx")
        l1_rows = [sem(f"l1_rows{u}") for u in range(2 * SLOTS1)]
        l1_free = [sem(f"l1_free{u}") for u in range(2 * SLOTS1)]
        away_ready = sem("away_ready")
        away_used = sem("away_used")
        queries_ready = sem("queries_ready")
        keysT_ps = sem("keysT_ps")
        keysT_ready = sem("keysT_ready")
        score_ps = sem("score_ps")
        max_ready = sem("max_ready")
        prob_ready = sem("prob_ready")
        probT_ps = sem("probT_ps")
        prob_copied = sem("prob_copied")
        spread_ready = sem("spread_ready")
        rep_ps = sem("rep_ps")
        part_ps = sem("part_ps")
        delta_ready = sem("delta_ready")
        factor_ready = sem("factor_ready")
        l1_vec = sem("l1_vec")
        l1_taken = sem("l1_taken")
        l1_reset = sem("l1_reset")
        x1_loaded = [sem(f"x1_loaded{k}") for k in range(SLOTS1)]
        attn_ready = sem("attn_ready")
        attn_ps = sem("attn_ps")
        group_vec = sem("group_vec")
        group_var = sem("group_var")
        group_std = sem("group_std")
        y_ready = sem("y_ready")
        y_stored = [sem(f"y_stored{k}") for k in range(SLOTS1)]

        block = ctx.enter_context(nc.Block())

        def gate(e, s, value):
            e.wait_ge(s, value)
            e.sem_inc(gates_passed, 1)

        def passes(e):
            e.wait_ge(passes_ready, 1)
            return e.value_load(passes_i[0:1, 0:1], min_val=1, max_val=NPASS)

        PAIRS = [-(-(TILES - v) // 2) for v in range(2)]
        TURNS = [-(-(NBLK - u) // SLOTS1) for u in range(SLOTS1)]

        def first_sweep(e, ps_, body, end):
            def pair_(i, v, half):
                return Pair(ps_ * NBLK + i * 2, i * 2, v, ps_ * PAIRS[v] + half, half)

            def tile(t, k, half):
                return Tile(ps_ * TILES + t, t, k, ps_ * PAIRS[k] + half)

            body(pair_(0, 0, 0), None)
            with e.Fori(0, (TILES - 1) // 2) as q:
                body(pair_(q * 2 + 1, 1, q), tile(q * 2, 0, q))
                body(pair_(q * 2 + 2, 0, q + 1), tile(q * 2 + 1, 1, q))
            end(tile(TILES - 1, 0, TILES // 2))

        def second_sweep(e, ps_, body):
            def blk(b, u, turn):
                return Block(ps_ * NBLK + b, b, u, ps_ * TURNS[u] + turn, turn)

            def step(i, v, group):
                u = (v + 1) % SLOTS1
                body(blk(i * SLOTS1 + v + 1, u, i + (v + 1) // SLOTS1), blk(i * SLOTS1 + v, v, i), group)

            body(blk(0, 0, 0), None, None)
            for v in range(SLOTS1):
                step(0, v, nodes(ps_, 0, 0, 0) if v == 2 else None)
            with e.Fori(1, NBLK // SLOTS1) as i:
                for v in range(SLOTS1):
                    step(i, v, nodes(ps_, i * SLOTS1 + v - 2, (v + 1) % SLOTS1, i - 1 + (v + 1) // SLOTS1))
            last = NBLK // SLOTS1
            body(blk(NBLK - 1, 1, last), blk(NBLK - 2, 0, last), nodes(ps_, GROUPS - 4, 1, last - 1))
            body(None, blk(NBLK - 1, 1, last), nodes(ps_, GROUPS - 3, 2, last - 1))
            for g in range(GROUPS - 2, GROUPS):
                body(None, None, nodes(ps_, g, g % SLOTS1, g // SLOTS1))

        def nodes(ps_, g, k, turn):
            return Group(ps_ * GROUPS + g, g, k, ps_ * TURNS[k] + turn)

        def load_edges(e, tile, dram, s):
            e.dma_start(tile[:, 0:FULL * RUN].rearrange("p (h j) -> p h j", j=RUN),
                        dram[0:FULL * HALF].rearrange("(h p j) -> p h j", p=P, j=RUN)).then_inc(s, 16)
            e.dma_start(tile[0:REST // RUN, FULL * RUN:EDGE_COLS],
                        dram[FULL * HALF:E].rearrange("(p j) -> p j", j=RUN)).then_inc(s, 16)

        @block.sync
        def _(sp):
            sp.wait_ge(pads_ready, 3)
            load_edges(sp, dst_i, dst, L["dst"])
            load_edges(sp, src_idx[:, 0:EDGE_COLS].bitcast(I32), src, L["src"])
            sp.wait_ge(L["src"], 32)
            load_edges(sp, etype_i, etype, L["etype"])
            for w_s, w in ((wq_s, wq), (wk_s, wk), (wv_s, wv), (we_s, we)):
                sp.dma_start(w_s, w.rearrange("t i o -> i t o")).then_inc(L["weights"], 16)
            for k in range(2):
                sp.sem_inc(row_stored[k], 16)
                sp.sem_inc(x1_stored[k], 16)
            count = passes(sp)

            def load_x(t, k, rows=P):
                sp.dma_start(x_tile[k][0:rows, :], x[bass.ds(t * P, rows), :]).then_inc(x_loaded[k], 16)

            def store(tile):
                gate(sp, x1_ready, tile.n + 1)
                sp.dma_start(x1_dram[bass.ds(tile.t * P, P), :], x1_tile[tile.k]).then_inc(x1_stored[tile.k], 16)
                gate(sp, kw_low, tile.n + 1)
                gate(sp, kw_high, tile.n + 1)
                sp.dma_start(table_rows[bass.ds(tile.t * P, P), :], kv_rows[tile.k].rearrange("p e c -> p (e c)")
                             ).then_inc(row_stored[tile.k], 16)

            with sp.Fori(0, count) as ps_:
                load_x(0, 0)
                with sp.Fori(0, (TILES - 3) // 2) as q:
                    for k in range(2):
                        load_x(q * 2 + k + 1, 1 - k)
                        store(Tile(ps_ * TILES + q * 2 + k, q * 2 + k, k, None))
                for t in range(TILES - 3, TILES):
                    if t + 1 < TILES:
                        load_x(t + 1, (t + 1) % 2, P if t + 2 < TILES else LAST)
                    store(Tile(ps_ * TILES + t, t, t % 2, None))

            for k in range(2):
                sp.wait_ge(row_stored[k], count * (16 * PAIRS[k]) + 16)
                sp.wait_ge(x1_stored[k], count * (16 * PAIRS[k]) + 16)
            sp.sem_inc(l1_start, 1)

            def load_group(g, k):
                sp.dma_start(x1_group[k], x1_dram[bass.ds(g * WIN, WIN), :]).then_inc(x1_loaded[k], 16)

            def store_group(group, rows=WIN):
                gate(sp, y_ready, group.n + 1)
                sp.dma_start(out[bass.ds(group.g * WIN, rows), :], y_group[group.k][0:rows, :]
                             ).then_inc(y_stored[group.k], 16)

            for k in range(SLOTS1):
                sp.sem_inc(y_stored[k], 16)
            with sp.Fori(0, count) as ps_:
                load_group(0, 0)
                with sp.Fori(0, GROUPS // SLOTS1) as i:
                    for k in range(SLOTS1):
                        load_group(i * SLOTS1 + k + 1, (k + 1) % SLOTS1)
                        store_group(nodes(ps_, i * SLOTS1 + k, k, 0))
                load_group(GROUPS - 1, 1)
                store_group(nodes(ps_, GROUPS - 2, 0, 0))
                store_group(nodes(ps_, GROUPS - 1, 1, 0), LAST_GROUP)
            for k in range(SLOTS1):
                gate(sp, y_stored[k], count * (16 * TURNS[k]) + 16)

        @block.gpsimd
        def _(pool):
            tail = slice(FULL * RUN, EDGE_COLS)
            pool.memset(dst_i[:, tail], -4096).then_inc(pads_ready, 1)
            pool.memset(src_idx[:, FULL * RUN:], 0).then_inc(pads_ready, 1)
            pool.memset(etype_i[:, tail], 0).then_inc(pads_ready, 1)
            pool.iota(iota_i[:, :], pattern=[[1, WIN]], base=0, channel_multiplier=0).then_inc(consts_ready, 1)
            pool.iota(bound_i[:, :], pattern=[[WIN, NBLK], [0, 2]], base=-WIN, channel_multiplier=0
                      ).then_inc(consts_ready, 1)
            pool.memset(identf[:, :], 0.0).then_inc(pool_step, 1)
            pool.wait_ge(pool_step, 1)
            pool.affine_select(out=identf[:, :], in_=identf[:, :], compare_op=ALU.not_equal, fill=1.0, base=0,
                               pattern=[[-1, P]], channel_multiplier=1).then_inc(consts_ready, 1)
            pool.memset(onesf[:, :], 1.0).then_inc(consts_ready, 1)
            pool.memset(onesb[:, :], 1.0).then_inc(consts_ready, 1)
            pool.memset(eps_col[:, :], LN_EPS).then_inc(consts_ready, 1)
            pool.memset(key_idx[:, EDGE_COLS:], 0).then_inc(consts_ready, 1)
            pool.memset(queries_all[:, NPAD:NACC], 0.0).then_inc(consts_ready, 1)
            pool.dma_start(ntype_i[:, 0:TILES - 1], ntype[0:(TILES - 1) * P].rearrange("(t p) -> p t", p=P),
                           allow_slow_non_contiguous=True).then_inc(L["small"], 16)
            pool.dma_start(ntype_i[0:LAST, TILES - 1:TILES], ntype[(TILES - 1) * P:N].rearrange("(p t) -> p t", t=1)
                           ).then_inc(L["small"], 16)
            pool.dma_start(bias_c[:, :], b0.rearrange("(d a) -> d a", a=1)).then_inc(L["small"], 16)
            pool.dma_start(mu_b[:, :], mu.rearrange("(a d) -> a d", a=1).broadcast_to([P, ET])).then_inc(L["small"], 16)
            count = passes(pool)

            def gather(rows, table_, j, u, s):
                pool.indirect_dma_start(rows[u][:, j, :], None, table_,
                                        bass.IndirectOffsetOnAxis(ap=stage[:, u, j:j + 1], axis=0)).then_inc(s, 16)

            def l0(ps_, i, u):
                gate(pool, l0_idx, ps_ * (TILES + 1) + i * 2 + u // 2 + 1)
                gate(pool, l0_free[u], ps_ * PAIRS[u // 2] + i + 1)
                for j in range(COLS):
                    gather(x_ring, x, j, u, l0_rows[2 * u + j // RUN])

            def l1(ps_, i, u):
                gate(pool, l1_idx, ps_ * (NBLK + 2) + i * SLOTS1 + u + 1)
                for h in range(2):
                    gate(pool, l1_free[2 * u + h], ps_ * TURNS[u] + i + 1)
                    for j in range(RUN):
                        gather(kv_ring, table, h * RUN + j, u, l1_rows[2 * u + h])

            for slots, body, rows, taken, reset in ((SLOTS0, l0, l0_rows, l0_taken, l0_reset),
                                                    (SLOTS1, l1, l1_rows, l1_taken, l1_reset)):
                pool.sem_inc(reset, 1)
                with pool.Fori(0, count) as ps_:
                    with pool.Fori(0, NBLK // slots) as i:
                        for u in range(slots):
                            body(ps_, i, u)
                    for u in range(NBLK % slots):
                        body(ps_, NBLK // slots, u)
                    gate(pool, taken, ps_ + 1)
                    pool.inc_swdge_sem(rows, [16 * RUN * -(-(NBLK - k // 2) // slots) for k in range(2 * slots)],
                                       mode="sub")
                    pool.sem_inc(reset, 1)
                if body is l0:
                    pool.wait_ge(l1_start, 1)

        @block.tensor
        def _(pe):
            pe.wait_ge(consts_ready, 8)
            pe.wait_ge(L["w0"], 16)
            pe.transpose(bank[2][:, 0:P], w0_s[:, 0:D], identf[:, :])
            pe.transpose(bank[2][:, P:2 * P], w0_s[:, D:2 * D], identf[:, :]).then_inc(w0_ps, 1)
            pe.wait_ge(dst_ready, 1)
            pe.matmul(bank[0][:, 0:NHALF], onesf[0:1, :],
                      dst_f[0:1, :].rearrange("p (h j) -> p h j", j=RUN)[:, :, 0], start=True, stop=True
                      ).then_inc(first_ps, 1)
            pe.wait_ge(inside_ready, 1)
            pe.matmul(bank[1][:, 0:1], onesf[:, :], plan[:, 0:1], start=True, stop=True).then_inc(inside_ps, 1)
            pe.wait_ge(w0_ready, 1)
            pe.wait_ge(L["weights"], 64)
            count = passes(pe)

            def sum_block(pair_, o):
                u = 2 * pair_.v + o
                pe.wait_ge(hot_ready, pair_.it + o + 1)
                for h in range(2):
                    pe.wait_ge(l0_rows[2 * u + h], (pair_.here + 1) * (16 * RUN))
                    for what in range(2):
                        at = (h * 2 + what) * WIN
                        for j in range(RUN):
                            mm = pe.matmul(bank[o][:, at:at + WIN],
                                           onesb[:, :] if what else x_ring[u][:, h * RUN + j, :],
                                           (hot_b if what else hot)[o][:, h * RUN + j, :],
                                           start=(j == 0), stop=(j == RUN - 1))
                mm.then_inc(l0_part, 1)

            def transpose_x(tile):
                pe.wait_ge(x_loaded[tile.k], (tile.turn + 1) * 16)
                pe.transpose(bank[2][:, 0:P], x_tile[tile.k], identf[:, :]).then_inc(xT_ps, 1)

            def first_product(tile):
                pe.wait_ge(xT_copied, tile.n + 1)
                pe.wait_ge(mean_ready, tile.n + 1)
                pe.matmul(bank[2][:, 0:P], w0T[:, 0, :], xT, start=True, stop=False)
                pe.matmul(bank[2][:, 0:P], w0T[:, 1, :], meanT, start=False, stop=True).then_inc(reluT_ps, 1)

            def transpose_relu(tile):
                pe.wait_ge(relu_ready, tile.n + 1)
                pe.transpose(bank[2][:, 0:P], reluT, identf[:, :]).then_inc(relu_ps, 1)

            def transpose_typed(tile):
                pe.wait_ge(typed_ready, tile.n + 1)
                for t in range(NT):
                    tr = pe.transpose(bank[3][:, t * P:(t + 1) * P], x1_typed[:, t, :], identf[:, :])
                tr.then_inc(typedT_ps, 1)

            def project_keys(tile):
                pe.wait_ge(typedT_ready, tile.n + 1)
                for t in range(NT):
                    mm = pe.matmul(bank[4][:, 0:P], wk_s[:, t, :], x1_typedT[:, t, :], start=(t == 0), stop=(t == NT - 1))
                mm.then_inc(k_ps, 1)
                for t in range(NT):
                    mm = pe.matmul(bank[6][:, 0:P], x1_typedT[:, t, :], wv_s[:, t, :], start=(t == 0), stop=(t == NT - 1))
                mm.then_inc(v_ps, 1)

            def project_queries(tile):
                for t in range(NT):
                    mm = pe.matmul(bank[5][:, 0:P], wq_s[:, t, :], x1_typedT[:, t, :], start=(t == 0), stop=(t == NT - 1))
                mm.then_inc(q_ps, 1)

            def edge_keys(tile):
                pe.wait_ge(kT_ready, tile.n + 1)
                pe.matmul(bank[7], kT, we_s[:, 0:4, :], start=True, stop=True)
                pe.matmul(bank[3], kT, we_s[:, 4:8, :], start=True, stop=True).then_inc(kw_ps, 1)

            def tile_products(tile):
                transpose_x(tile)
                first_product(tile)
                transpose_relu(tile)
                transpose_typed(tile)
                project_keys(tile)
                edge_keys(tile)

            def l0(pair_, tile):
                sum_block(pair_, 0)
                if tile:
                    tile_products(tile)
                sum_block(pair_, 1)
                if tile:
                    project_queries(tile)

            def l0_end(tile):
                tile_products(tile)
                project_queries(tile)

            with pe.Fori(0, count) as ps_:
                gate(pe, l0_reset, ps_ + 1)
                first_sweep(pe, ps_, l0, l0_end)
                pe.sem_inc(l0_taken, 1)

            scores, probs = pair[1], pair[2]

            def mask(new):
                pe.wait_ge(away_ready, new.it + 1)
                for h in range(2):
                    for q in range(2):
                        for j in range(4):
                            at = q * 512 + j * P
                            mm = pe.matmul(scores[h * WIN:(h + 1) * WIN, at:at + P], away[:, h * RUN + q * 4 + j, :],
                                           negid[:, :], start=(j == 0), stop=False, skip_group_check=True)
                mm.then_inc(away_used, 1)

            def score(old):
                pe.wait_ge(queries_ready, old.it + 1)
                for g in range(4):
                    h, q = g // 2, g % 2
                    pe.wait_ge(keysT_ready, old.it * 4 + g + 1)
                    mm = pe.matmul(scores[h * WIN:(h + 1) * WIN, q * 512:(q + 1) * 512], queries[:, h, :],
                                   keysT[:, g, :], start=False, stop=True, skip_group_check=True)
                mm.then_inc(score_ps, 1)

            def transpose_keys(new, h):
                pe.wait_ge(l1_rows[2 * new.u + h], (new.here + 1) * (16 * RUN))
                for g in range(2 * h, 2 * h + 2):
                    if g >= 2:
                        pe.wait_ge(keysT_ready, new.it * 4 + g - 1)
                    for j in range(4):
                        tr = pe.transpose(bank[g % 2][:, j * P:(j + 1) * P], kv_ring[new.u][:, g * 4 + j, 0:D],
                                          identf[:, :])
                    tr.then_inc(keysT_ps, 1)

            def attn_rows(group):
                pe.wait_ge(attn_ready, group.n + 1)
                pe.matmul(bank[4][0:WIN, 0:P], attnT, identf[:, :], start=True, stop=True).then_inc(attn_ps, 1)

            def l1(new, old, group):
                if old:
                    score(old)
                if new:
                    transpose_keys(new, 0)
                if old:
                    pe.wait_ge(prob_ready, old.it + 1)
                    for j in range(RUN):
                        tr = pe.transpose(probs[:, j * P:(j + 1) * P], probT[:, j * P:(j + 1) * P], identf[:, :])
                    tr.then_inc(probT_ps, 1)
                    pe.wait_ge(spread_ready, old.it + 1)
                    pe.matmul(maxima, onesf[:, :], spread[:, 0, :], start=True, stop=True)
                    for h in (1, 0):
                        mm = pe.matmul(part[h][:, WIN:2 * WIN], onesf[:, :], spread[:, 1, h * WIN:(h + 1) * WIN],
                                       start=True, stop=True)
                        if h:
                            mm.then_inc(rep_ps, 1)
                if new:
                    mask(new)
                if old:
                    pe.wait_ge(prob_copied, old.it * 2 + 2)
                if group:
                    attn_rows(group)
                if old:
                    for h in range(2):
                        if h:
                            pe.wait_ge(delta_ready, old.it * 2 + 2)
                        for j in range(RUN):
                            mm = pe.matmul(part[h][:, 0:WIN], kv_ring[old.u][:, h * RUN + j, D:2 * D],
                                           prob[:, j, h * WIN:(h + 1) * WIN], start=(j == 0), stop=(j == RUN - 1))
                        mm.then_inc(part_ps, 1)
                if new:
                    transpose_keys(new, 1)

            with pe.Fori(0, count) as ps_:
                gate(pe, l1_reset, ps_ + 1)
                second_sweep(pe, ps_, l1)
                pe.sem_inc(l1_taken, 1)

        @block.scalar
        def _(act):
            act.dma_start(w0_s, w0[:, :]).then_inc(L["w0"], 16)
            act.wait_ge(w0_ps, 1)
            act.activation(w0T[:, :, :], by_type(bank[2][:, 0:2 * P]), ACT.Copy).then_inc(w0_ready, 1)
            act.wait_ge(L["small"], 64)
            act.wait_ge(L["src"], 32)
            count = passes(act)

            def copy_x(tile):
                act.wait_ge(xT_ps, tile.n + 1)
                act.activation(xT, bank[2][:, 0:P], ACT.Copy).then_inc(xT_copied, 1)

            def relu(tile):
                act.wait_ge(reluT_ps, tile.n + 1)
                act.activation(reluT, bank[2][:, 0:P], ACT.Relu, bias=bias_c[:, 0:1]).then_inc(relu_ready, 1)

            def deviation(tile):
                act.wait_ge(var_ready, tile.n + 1)
                act.activation(rstd[:, :], aggr[:, 1:2], ACT.Sqrt, bias=eps_col[:, 0:1]).then_inc(std_ready, 1)

            def copy_typed(tile):
                act.wait_ge(typedT_ps, tile.n + 1)
                act.activation(x1_typedT, by_type(bank[3]), ACT.Copy).then_inc(typedT_ready, 1)

            def copy_projected(tile):
                act.wait_ge(k_ps, tile.n + 1)
                act.activation(kT, bank[4][:, 0:P], ACT.Copy).then_inc(kT_ready, 1)
                act.wait_ge(row_stored[tile.k], (tile.turn + 1) * 16)
                act.wait_ge(v_ps, tile.n + 1)
                act.activation(kv_rows[tile.k][:, :, D:2 * D], bank[6][:, 0:P].unsqueeze(1).broadcast_to([P, ET, D]),
                               ACT.Copy)

            def copy_queries(tile):
                act.wait_ge(q_ps, tile.n + 1)
                act.activation(queries_all[:, bass.ds(tile.t * P, P)], bank[5][:, 0:P], ACT.Copy).then_inc(q_copied, 1)

            def copy_high(tile):
                act.wait_ge(kw_ps, tile.n + 1)
                act.activation(kv_rows[tile.k][:, 4:8, 0:D], by_type(bank[3]), ACT.Copy).then_inc(kw_high, 1)

            def stage_pair(v, b):
                act.activation(stage[:, 2 * v:2 * v + 2, :].bitcast(I32).rearrange("p a b -> p (a b)"),
                               src_idx[:, bass.ds(b * COLS, 2 * COLS)].bitcast(I32), ACT.Copy).then_inc(l0_idx, 1)

            def finish_tile(tile):
                copy_x(tile)
                relu(tile)
                deviation(tile)
                copy_typed(tile)
                copy_projected(tile)
                copy_high(tile)
                copy_queries(tile)

            def next_pair(pair_):
                if not isinstance(pair_.b, int) or pair_.b > 0:
                    gate(act, l0_part, pair_.it)
                stage_pair(1 - pair_.v, pair_.b + 2)

            def l0(pair_, tile):
                next_pair(pair_)
                if tile:
                    finish_tile(tile)

            with act.Fori(0, count) as ps_:
                stage_pair(0, 0)
                first_sweep(act, ps_, l0, finish_tile)
            act.wait_ge(keys_ready, 1)

            def stage_block(u, b):
                act.activation(stage[:, u, :].bitcast(I32), key_idx[:, bass.ds(b * COLS, COLS)].bitcast(I32), ACT.Copy
                               ).then_inc(l1_idx, 1)

            def copy_keys(new, h):
                for g in range(2 * h, 2 * h + 2):
                    act.wait_ge(keysT_ps, new.it * 4 + g + 1)
                    act.activation(keysT[:, g, :], bank[g % 2], ACT.Copy).then_inc(keysT_ready, 1)

            def l1(new, old, group):
                if new:
                    stage_block((new.u + 2) % SLOTS1, new.b + 2)
                if old:
                    act.wait_ge(max_ready, old.it + 1)
                    act.activation(probT[:, :], pair[1], ACT.Exp, bias=cols[:, 1:2], accum_out=cols[:, 2:3]
                                   ).then_inc(prob_ready, 1)
                if new:
                    copy_keys(new, 0)
                if old:
                    act.wait_ge(probT_ps, old.it + 1)
                    act.activation(prob[:, 0:4, :].rearrange("p a b -> p (a b)"), bank[4], ACT.Copy).then_inc(prob_copied, 1)
                    act.wait_ge(delta_ready, old.it * 2 + 2)
                    act.activation(factor[:, :, :, :], delta[:, :, :, :], ACT.Exp).then_inc(factor_ready, 1)
                if group:
                    act.wait_ge(group_var, group.n + 1)
                    act.activation(rstd[0:WIN, :], aggr[0:WIN, 1:2], ACT.Sqrt, bias=eps_col[0:WIN, 0:1]
                                   ).then_inc(group_std, 1)
                if new:
                    copy_keys(new, 1)

            with act.Fori(0, count) as ps_:
                stage_block(0, 0)
                stage_block(1, 1)
                second_sweep(act, ps_, l1)

        @block.vector
        def _(dve):
            steps = [0]

            def setup(ins):
                steps[0] += 1
                ins.then_inc(setup_vec, 1)
                dve.wait_ge(setup_vec, steps[0])

            edges = lambda t: t.rearrange("p (h j) -> p h j", j=RUN)
            over = lambda t: t[:, :].unsqueeze(2).broadcast_to([P, NHALF, RUN])
            dve.wait_ge(L["dst"], 32)
            setup(dve.tensor_copy(dst_f[:, :], dst_i))
            dve.sem_inc(dst_ready, 1)
            dve.wait_ge(consts_ready, 8)
            dve.tensor_copy(iota_f[:, :], iota_i[:, :])
            dve.tensor_scalar(negid[:, :], identf[:, :], NEG, None, ALU.mult)
            dve.memset(plan[:, 3:4], 0.0)
            dve.wait_ge(first_ps, 1)
            setup(dve.tensor_copy(first[:, :], bank[0][:, 0:NHALF]))
            test, low = ring[:, 0:EDGE_COLS], base_f
            dve.tensor_tensor(low[:, :], first[:, :], bound_i[:, :], ALU.is_ge)
            setup(dve.tensor_tensor(edges(rel[:, :]), edges(dst_f[:, :]), over(first), ALU.subtract))
            setup(dve.tensor_scalar(test, rel[:, :], float(WIN), None, ALU.is_lt))
            setup(dve.scalar_tensor_tensor(test, rel[:, :], 0.0, test, ALU.is_ge, ALU.mult))
            setup(dve.tensor_tensor(edges(test), edges(test), over(low), ALU.mult))
            setup(dve.reduce_sum(plan[:, 0:1], test, AX))
            dve.sem_inc(inside_ready, 1)
            dve.wait_ge(inside_ps, 1)
            setup(dve.tensor_scalar(plan[:, 1:2], bank[1][:, 0:1], float(E), None, ALU.is_equal))
            dve.tensor_scalar(plan[:, 2:3], plan[:, 1:2], -float(WIN), float(WIN), ALU.mult, ALU.add)
            setup(dve.tensor_scalar(passes_i[0:1, 0:1], plan[0:1, 1:2], float(1 - NPASS), float(NPASS), ALU.mult, ALU.add))
            dve.sem_inc(passes_ready, 1)
            for u in range(SLOTS0):
                dve.sem_inc(l0_free[u], 1)
            count = passes(dve)
            dve.memset(sums[:, :, :], 0.0)
            dve.wait_ge(L["etype"], 32)
            dve.wait_ge(L["src"], 32)
            dve.wait_ge(L["small"], 64)
            dve.wait_ge(L["weights"], 64)
            dve.scalar_tensor_tensor(key_idx[:, 0:EDGE_COLS], src_idx[:, 0:EDGE_COLS].bitcast(I32), float(ET), etype_i,
                                     ALU.mult, ALU.add)
            setup(dve.memset(ntype_m[:, TILES - 1, :], 0.0))
            for t in range(NT):
                dve.tensor_scalar(ntype_m[:, 0:TILES - 1, t], ntype_i[:, 0:TILES - 1], float(t), None, ALU.is_equal)
                dve.tensor_scalar(ntype_m[0:LAST, TILES - 1, t:t + 1], ntype_i[0:LAST, TILES - 1:TILES], float(t), None,
                                  ALU.is_equal)
            for e in range(ET):
                ins = dve.tensor_scalar(we_s[:, e, :], we_s[:, e, :], mu_b[:, e:e + 1], SCALE, ALU.mult, ALU.mult)
            setup(ins)
            dve.sem_inc(keys_ready, 1)
            dve.sem_inc(l0_added, 1)

            def tables(chain, ps_):
                dve.scalar_tensor_tensor(base_f[:, :], first[:, :], plan[:, 1:2],
                                         plan[:, 3:4].broadcast_to([P, NHALF]), ALU.mult, ALU.add).then_inc(chain, 1)
                dve.wait_ge(chain, ps_ * 3 + 1)
                dve.tensor_scalar(plan[:, 3:4], plan[:, 3:4], plan[:, 2:3], None, ALU.add).then_inc(chain, 1)
                dve.tensor_copy(base_i[0:1, :], base_f[0:1, :])
                dve.tensor_tensor(edges(rel[:, :]), edges(dst_f[:, :]), over(base_f), ALU.subtract).then_inc(chain, 1)
                gate(dve, chain, ps_ * 3 + 3)

            def member(out_, b, op):
                return dve.tensor_tensor(
                    out_, rel[:, bass.ds(b * COLS, COLS)].unsqueeze(2).broadcast_to([P, COLS, WIN]),
                    iota_f[:, :].unsqueeze(1).broadcast_to([P, COLS, WIN]), op)

            def bases(b):
                return [dve.value_load(base_i[0:1, bass.ds(b * 2 + h, 1)], min_val=0, max_val=NPAD) for h in range(2)]

            def find_nodes(pair_, o):
                member(hot_b[o], pair_.b + o, ALU.is_equal)
                member(hot[o], pair_.b + o, ALU.is_equal).then_inc(hot_ready, 1)

            def add_block(pair_, o):
                base = bases(pair_.b + o)
                dve.wait_ge(l0_part, pair_.it + o + 1)
                dve.sem_inc(l0_free[2 * pair_.v + o], 1)
                for h in range(2):
                    dve.wait_ge(l0_added, (pair_.it + o) * 2 + h + 1)
                    win = sums[:, :, bass.ds(base[h], WIN)]
                    dve.tensor_tensor(win, bank[o][:, h * 2 * WIN:(h + 1) * 2 * WIN].rearrange("p (a w) -> p a w", w=WIN),
                                      win, ALU.add).then_inc(l0_added, 1)

            def mean(tile, added):
                w = bass.ds(tile.t * P, P)

                def link(ins, k):
                    ins.then_inc(tile_vec, 1)
                    dve.wait_ge(tile_vec, tile.n * 6 + k)
                dve.wait_ge(l0_added, added)
                link(dve.tensor_scalar(inverse, sums[:, 1, w], 1.0, None, ALU.max), 1)
                link(dve.reciprocal(inverse, inverse), 2)
                dve.tensor_tensor(summed, sums[:, 0, w], inverse, ALU.mult)
                dve.wait_ge(xT_copied, tile.n + 1)
                link(dve.scalar_tensor_tensor(alone, sums[:, 1, w], 0.0, xT, ALU.is_equal, ALU.mult), 3)
                dve.tensor_tensor(meanT, summed, alone, ALU.add).then_inc(mean_ready, 1)

            def norm_x1(tile):
                def link(ins, k):
                    ins.then_inc(tile_vec, 1)
                    dve.wait_ge(tile_vec, tile.n * 6 + k)
                dve.wait_ge(relu_ps, tile.n + 1)
                link(dve.tensor_tensor(summed, bank[2][:, 0:P], x_tile[tile.k], ALU.add), 4)
                dve.bn_stats(stats[:, :], summed).then_inc(tile_vec, 1)
                gate(dve, tile_vec, tile.n * 6 + 5)
                dve.bn_aggr(aggr[:, :], stats[:, :]).then_inc(var_ready, 1)
                dve.wait_ge(std_ready, tile.n + 1)
                link(dve.reciprocal(rstd[:, :], rstd[:, :]), 6)
                dve.wait_ge(x1_stored[tile.k], (tile.turn + 1) * 16)
                dve.tensor_scalar(x1_tile[tile.k], summed, aggr[:, 0:1], rstd[:, 0:1], ALU.subtract, ALU.mult
                                  ).then_inc(x1_ready, 1)
                dve.wait_ge(x1_ready, tile.n + 1)
                for t in range(NT):
                    m = ntype_m[:, bass.ds(tile.t, 1), t:t + 1].rearrange("p a b -> p (a b)")
                    ins = dve.tensor_scalar(x1_typed[:, t, :], x1_tile[tile.k], m, None, ALU.mult)
                ins.then_inc(typed_ready, 1)

            def copy_rows(tile):
                dve.wait_ge(kw_ps, tile.n + 1)
                dve.wait_ge(row_stored[tile.k], (tile.turn + 1) * 16)
                dve.tensor_copy(kv_rows[tile.k][:, 0:4, 0:D], by_type(bank[7])).then_inc(kw_low, 1)

            with dve.Fori(0, count) as ps_:
                tables(l0_tables, ps_)

                def l0(pair_, tile):
                    find_nodes(pair_, 0)
                    find_nodes(pair_, 1)
                    add_block(pair_, 0)
                    if tile:
                        finish_tile(tile, pair_.it * 2 + 3)
                    add_block(pair_, 1)

                def finish_tile(tile, added):
                    mean(tile, added)
                    norm_x1(tile)
                    copy_rows(tile)

                def l0_end(tile):
                    finish_tile(tile, (ps_ + 1) * (2 * NBLK) + 1)

                first_sweep(dve, ps_, l0, l0_end)

            for u in range(2 * SLOTS1):
                dve.sem_inc(l1_free[u], 1)
            dve.memset(sums[:, :, :], 0.0)
            setup(dve.memset(plan[:, 3:4], 0.0))
            dve.sem_inc(away_used, 1)

            def group_link(group, ins, j):
                ins.then_inc(group_vec, 1)
                dve.wait_ge(group_vec, group.n * 5 + j)

            def divide(group):
                win = bass.ds(group.g * WIN, WIN)
                group_link(group, dve.tensor_scalar(attn_inverse, sums[:, 1, win], SUM_EPS, None, ALU.add), 1)
                group_link(group, dve.reciprocal(attn_inverse, attn_inverse), 2)
                dve.tensor_tensor(attnT, sums[:, 0, win], attn_inverse, ALU.mult).then_inc(attn_ready, 1)

            def finish(group):
                dve.wait_ge(x1_loaded[group.k], (group.turn + 1) * 16)
                dve.sem_inc(gates_passed, 1)
                dve.wait_ge(attn_ps, group.n + 1)
                group_link(group, dve.tensor_tensor(y_sum, bank[4][0:WIN, 0:P], x1_group[group.k], ALU.add), 3)
                dve.bn_stats(stats[0:WIN, :], y_sum).then_inc(group_vec, 1)
                gate(dve, group_vec, group.n * 5 + 4)
                dve.bn_aggr(aggr[0:WIN, :], stats[0:WIN, :]).then_inc(group_var, 1)
                dve.wait_ge(group_std, group.n + 1)
                group_link(group, dve.reciprocal(rstd[0:WIN, :], rstd[0:WIN, :]), 5)
                dve.wait_ge(y_stored[group.k], (group.turn + 1) * 16)
                dve.tensor_scalar(y_group[group.k], y_sum, aggr[0:WIN, 0:1], rstd[0:WIN, 0:1], ALU.subtract, ALU.mult
                                  ).then_inc(y_ready, 1)

            def l1(new, old, group):
                K = 9
                k = [0]

                def link(ins):
                    k[0] += 1
                    ins.then_inc(l1_vec, 1)
                    dve.wait_ge(l1_vec, old.it * K + k[0])

                def take_queries():
                    new_base = bases(new.b)
                    for h in range(2):
                        ins = dve.tensor_copy(queries[:, h, :], queries_all[:, bass.ds(new_base[h], WIN)])
                    ins.then_inc(queries_ready, 1)

                def mark_away(it, b):
                    dve.wait_ge(away_used, it + 1)
                    member(away[:, :, :], b, ALU.not_equal).then_inc(away_ready, 1)

                if not old:
                    if group:
                        divide(group)
                        finish(group)
                    else:
                        mark_away(new.it, 0)
                        take_queries()
                        mark_away(new.it + 1, 1)
                    return
                dve.wait_ge(score_ps, old.it + 1)
                link(dve.reduce_max(cols[:, 0:1], pair[1], AX))
                dve.tensor_scalar(cols[:, 1:2], cols[:, 0:1], FLOOR, -1.0, ALU.max, ALU.mult).then_inc(max_ready, 1)
                dve.wait_ge(max_ready, old.it + 1)
                dve.tensor_scalar(spread[:, 0, :], identf[:, :], cols[:, 1:2], None, ALU.mult)
                if new:
                    take_queries()
                dve.wait_ge(prob_ready, old.it + 1)
                dve.tensor_scalar(spread[:, 1, :], identf[:, :], cols[:, 2:3], None, ALU.mult).then_inc(spread_ready, 1)
                if group:
                    divide(group)
                dve.wait_ge(probT_ps, old.it + 1)
                dve.tensor_copy(prob[:, 4:8, :].rearrange("p a b -> p (a b)"), bank[5]).then_inc(prob_copied, 1)
                base = bases(old.b)
                dve.wait_ge(rep_ps, old.it + 1)
                for h in range(2):
                    win = bass.ds(base[h], WIN)
                    new_max = maxima[:, h * WIN:(h + 1) * WIN]
                    link(dve.tensor_tensor(larger[:, :], new_max, negmax[:, win], ALU.min))
                    dve.tensor_tensor(delta[:, h, 0, :], larger[:, :], negmax[:, win], ALU.subtract)
                    dve.tensor_tensor(delta[:, h, 1, :], larger[:, :], new_max, ALU.subtract).then_inc(delta_ready, 1)
                    gate(dve, delta_ready, old.it * 2 + h + 1)
                    link(dve.tensor_copy(negmax[:, win], larger[:, :]))
                if new and not (isinstance(new.b, int) and new.b == NBLK - 1):
                    mark_away(new.it + 1, new.b + 1)
                if group:
                    finish(group)
                dve.wait_ge(factor_ready, old.it + 1)
                for h in range(2):
                    win = bass.ds(base[h], WIN)
                    dve.tensor_tensor(scaled[:, 0, :, :], sums[:, :, win],
                                      factor[:, h, 0, :].unsqueeze(1).broadcast_to([P, 2, WIN]), ALU.mult)
                    dve.wait_ge(part_ps, old.it * 2 + h + 1)
                    dve.sem_inc(l1_free[2 * old.u + h], 1)
                    link(dve.tensor_tensor(scaled[:, 1, :, :],
                                           part[h].rearrange("p (a w) -> p a w", w=WIN),
                                           factor[:, h, 1, :].unsqueeze(1).broadcast_to([P, 2, WIN]), ALU.mult))
                    link(dve.tensor_tensor(sums[:, :, win], scaled[:, 0, :, :], scaled[:, 1, :, :], ALU.add))
                assert k[0] == K
                dve.sem_inc(gates_passed, 1)

            gate(dve, q_copied, count * TILES)
            dve.wait_ge(l1_start, 1)
            setup(dve.memset(negmax[:, :], -FLOOR))
            with dve.Fori(0, count) as ps_:
                tables(l1_tables, ps_)
                second_sweep(dve, ps_, l1)


_INS = ["x", "src", "dst", "edge_type_8", "node_type_4", "L0_gnn_W", "L0_gnn_b", "L1_gnn_W_Q", "L1_gnn_W_K",
        "L1_gnn_W_V", "L1_gnn_W_edge", "L1_gnn_mu"]


def kernel(**inputs):
    import numpy as _np
    import concourse.bacc as _bacc
    from concourse import mybir as _mybir
    from concourse.bass_utils import run_bass_kernel_spmd as _run

    nc = _bacc.Bacc("TRN2", target_bir_lowering=False, num_devices=1)
    arrays, args = {}, []
    for name in _INS:
        a = _np.ascontiguousarray(inputs[name])
        arrays[f"in_{name}_dram"] = a
        args.append(nc.dram_tensor(f"in_{name}_dram", a.shape, _mybir.dt.from_np(a.dtype), kind="ExternalInput").ap())
    args.append(nc.dram_tensor("out_0_dram", inputs["x"].shape, _mybir.dt.float32, kind="ExternalOutput").ap())
    gnn_kernel(nc, *args)
    r = _run(nc, [arrays], core_ids=[0])
    return r.results[0]["out_0_dram"]
```
